# Optimizing a Trainium2 kernel written in Bass

```python
import numpy as np
import jax
import jax.numpy as jnp

def _softmax(x, axis=-1):
    return jax.nn.softmax(x, axis=axis)

def _gelu(x):
    return jax.nn.gelu(x, approximate=True)

def _silu(x):
    return jax.nn.silu(x)

def _sigmoid(x):
    return jax.nn.sigmoid(x)

def _layernorm(x, axis=-1, eps=1e-05):
    m = jnp.mean(x, axis=axis, keepdims=True)
    v = jnp.var(x, axis=axis, keepdims=True)
    return (x - m) / jnp.sqrt(v + eps)

def _scatter_add(tgt, idx, src, axis=0):
    return tgt.at[idx].add(src)

def _segment_sum(src, seg, n):
    return jax.ops.segment_sum(src, seg, n)
kernel_name = 'mk_audio_tower_d2_tok_audfeat768_r4_a84fa1'

def setup_inputs(seed: int=0):
    np.random.seed(seed)
    _w = jnp.asarray

    def _rec_inputs():
        import jax
        import jax.numpy as jnp
        _rk = jax.random.key(seed)
        x = -0.000183583 + 0.999963 * jax.random.normal(jax.random.fold_in(_rk, 1), (16, 256, 192), jnp.float32)
        return x
    x = _rec_inputs()

    def _L0_tok_setup():
        import jax, jax.numpy as jnp
        import numpy as np
        KEEP_RATIO = 0.7
        key = jax.random.key(seed)
        kx, kw = jax.random.split(key)
        B, N, D = (32, 1024, 192)
        x = jax.random.normal(kx, (B, N, D), dtype=jnp.float32)
        w = jax.random.normal(kw, (D, 1), dtype=jnp.float32) * (1.0 / np.sqrt(D))
        b = jnp.zeros((1,), dtype=jnp.float32)
        return {'x': x, 'w': w, 'b': b}
    _L0_tok_all = _L0_tok_setup()
    _L0_tok_in = {k: v for k, v in _L0_tok_all.items() if k in ('w', 'b')}
    del _L0_tok_all

    def _L0_attn_setup():
        import jax, jax.numpy as jnp
        import numpy as np
        NUM_HEADS = 12

        def _shape(x, B, H, D):
            B_, S, _ = x.shape
            return x.reshape(B_, S, H, D).transpose(0, 2, 1, 3)
        key = jax.random.key(seed)
        ks = jax.random.split(key, 11)
        E = 192
        B, T = (1, 128)
        D = E // NUM_HEADS
        s = 0.02
        return {'hidden_states': jax.random.normal(ks[0], (B, T, E), jnp.float32), 'Wq': jax.random.normal(ks[1], (E, E), jnp.float32) * s, 'bq': jax.random.normal(ks[2], (E,), jnp.float32) * s, 'Wk': jax.random.normal(ks[3], (E, E), jnp.float32) * s, 'bk': jax.random.normal(ks[4], (E,), jnp.float32) * s, 'Wv': jax.random.normal(ks[5], (E, E), jnp.float32) * s, 'bv': jax.random.normal(ks[6], (E,), jnp.float32) * s, 'Wo': jax.random.normal(ks[7], (E, E), jnp.float32) * s, 'bo': jax.random.normal(ks[8], (E,), jnp.float32) * s, 'ws': jax.random.normal(ks[9], (D,), jnp.float32) * s, 'bs': jax.random.normal(ks[10], (1,), jnp.float32) * s}
    _L0_attn_all = _L0_attn_setup()
    _L0_attn_in = {k: v for k, v in _L0_attn_all.items() if k in ('Wq', 'bq', 'Wk', 'bk', 'Wv', 'bv', 'Wo', 'bo', 'ws', 'bs')}
    del _L0_attn_all

    def _L0_ffn_setup():
        import jax, jax.numpy as jnp
        import numpy as np

        def _fq(x, scale, qmin, qmax):
            q = jnp.clip(jnp.round(x / scale), qmin, qmax) * scale
            return x + jax.lax.stop_gradient(q - x)

        def _quant_weight(W):
            scale = jnp.max(jnp.abs(W)) / 127.0
            return _fq(W, scale, -127.0, 127.0)
        key = jax.random.key(seed)
        ks = jax.random.split(key, 5)
        B, S, D, H = (64, 196, 192, 768)
        x = jax.random.normal(ks[0], (B, S, D), dtype=jnp.float32)
        W1 = jax.random.normal(ks[1], (H, D), dtype=jnp.float32) * D ** (-0.5)
        b1 = jax.random.normal(ks[2], (H,), dtype=jnp.float32) * 0.01
        W2 = jax.random.normal(ks[3], (D, H), dtype=jnp.float32) * H ** (-0.5)
        b2 = jax.random.normal(ks[4], (D,), dtype=jnp.float32) * 0.01
        s_gelu = jnp.float32(0.05)
        s_out = jnp.float32(0.02)
        return {'x': x, 'W1': W1, 'b1': b1, 'W2': W2, 'b2': b2, 's_gelu': s_gelu, 's_out': s_out}
    _L0_ffn_all = _L0_ffn_setup()
    _L0_ffn_in = {k: v for k, v in _L0_ffn_all.items() if k in ('W1', 'b1', 'W2', 'b2', 's_gelu', 's_out')}
    del _L0_ffn_all

    def _L1_attn_setup():
        import jax, jax.numpy as jnp
        import numpy as np
        LOG2E = 1.4426950408889634
        NUM_HEADS = 12

        def fake_quant_sym8(x):
            scale = jnp.maximum(jnp.max(jnp.abs(x)) / 127.0, 1e-08)
            q = jnp.clip(jnp.round(x / scale), -128.0, 127.0) * scale
            return x + jax.lax.stop_gradient(q - x)

        def integer_approx_softmax(x):
            z = x * LOG2E
            z = z - jnp.max(z, axis=-1, keepdims=True)
            zi = jnp.floor(z)
            zf = z - zi
            p = jnp.exp2(zi) * (1.0 + zf)
            return p / jnp.sum(p, axis=-1, keepdims=True)
        key = jax.random.key(seed)
        ks = jax.random.split(key, 5)
        B, N, E, P = (8, 256, 192, 192)
        s = 0.02
        return {'x': jax.random.normal(ks[0], (B, N, E), jnp.float32), 'Wq': jax.random.normal(ks[1], (E, P), jnp.float32) * s, 'bq': jnp.zeros((P,), jnp.float32), 'Wk': jax.random.normal(ks[2], (E, P), jnp.float32) * s, 'bk': jnp.zeros((P,), jnp.float32), 'Wv': jax.random.normal(ks[3], (E, P), jnp.float32) * s, 'bv': jnp.zeros((P,), jnp.float32), 'Wo': jax.random.normal(ks[4], (P, E), jnp.float32) * s, 'bo': jnp.zeros((E,), jnp.float32)}
    _L1_attn_all = _L1_attn_setup()
    _L1_attn_in = {k: v for k, v in _L1_attn_all.items() if k in ('Wq', 'bq', 'Wk', 'bk', 'Wv', 'bv', 'Wo', 'bo')}
    del _L1_attn_all

    def _L1_ffn_setup():
        import jax, jax.numpy as jnp
        import numpy as np
        E, D, H = (16, 192, 192)
        B, N = (32, 197)
        key = jax.random.key(seed)
        ks = jax.random.split(key, 7)
        s = 0.02
        return {'x': jax.random.normal(ks[0], (B, N, D), dtype=jnp.float32), 'W1': jax.random.normal(ks[1], (E, H, D), dtype=jnp.float32) * s, 'b1': jax.random.normal(ks[2], (E, H), dtype=jnp.float32) * s, 'W2': jax.random.normal(ks[3], (E, D, H), dtype=jnp.float32) * s, 'b2': jax.random.normal(ks[4], (E, D), dtype=jnp.float32) * s, 'Wg': jax.random.normal(ks[5], (E, D), dtype=jnp.float32) * s, 'bg': jnp.zeros((E,), dtype=jnp.float32)}
    _L1_ffn_all = _L1_ffn_setup()
    _L1_ffn_in = {k: v for k, v in _L1_ffn_all.items() if k in ('W1', 'b1', 'W2', 'b2', 'Wg', 'bg')}
    del _L1_ffn_all
    return {'x': x, 'L0_tok_w': _L0_tok_in['w'], 'L0_tok_b': _L0_tok_in['b'], 'L0_attn_Wq': _L0_attn_in['Wq'], 'L0_attn_bq': _L0_attn_in['bq'], 'L0_attn_Wk': _L0_attn_in['Wk'], 'L0_attn_bk': _L0_attn_in['bk'], 'L0_attn_Wv': _L0_attn_in['Wv'], 'L0_attn_bv': _L0_attn_in['bv'], 'L0_attn_Wo': _L0_attn_in['Wo'], 'L0_attn_bo': _L0_attn_in['bo'], 'L0_attn_ws': _L0_attn_in['ws'], 'L0_attn_bs': _L0_attn_in['bs'], 'L0_ffn_W1': _L0_ffn_in['W1'], 'L0_ffn_b1': _L0_ffn_in['b1'], 'L0_ffn_W2': _L0_ffn_in['W2'], 'L0_ffn_b2': _L0_ffn_in['b2'], 'L0_ffn_s_gelu': _L0_ffn_in['s_gelu'], 'L0_ffn_s_out': _L0_ffn_in['s_out'], 'L1_attn_Wq': _L1_attn_in['Wq'], 'L1_attn_bq': _L1_attn_in['bq'], 'L1_attn_Wk': _L1_attn_in['Wk'], 'L1_attn_bk': _L1_attn_in['bk'], 'L1_attn_Wv': _L1_attn_in['Wv'], 'L1_attn_bv': _L1_attn_in['bv'], 'L1_attn_Wo': _L1_attn_in['Wo'], 'L1_attn_bo': _L1_attn_in['bo'], 'L1_ffn_W1': _L1_ffn_in['W1'], 'L1_ffn_b1': _L1_ffn_in['b1'], 'L1_ffn_W2': _L1_ffn_in['W2'], 'L1_ffn_b2': _L1_ffn_in['b2'], 'L1_ffn_Wg': _L1_ffn_in['Wg'], 'L1_ffn_bg': _L1_ffn_in['bg']}

def reference(x, L0_tok_w, L0_tok_b, L0_attn_Wq, L0_attn_bq, L0_attn_Wk, L0_attn_bk, L0_attn_Wv, L0_attn_bv, L0_attn_Wo, L0_attn_bo, L0_attn_ws, L0_attn_bs, L0_ffn_W1, L0_ffn_b1, L0_ffn_W2, L0_ffn_b2, L0_ffn_s_gelu, L0_ffn_s_out, L1_attn_Wq, L1_attn_bq, L1_attn_Wk, L1_attn_bk, L1_attn_Wv, L1_attn_bv, L1_attn_Wo, L1_attn_bo, L1_ffn_W1, L1_ffn_b1, L1_ffn_W2, L1_ffn_b2, L1_ffn_Wg, L1_ffn_bg):
    import jax
    import jax.numpy as jnp

    def _L0_tok_ref(x, w, b):
        import jax, jax.numpy as jnp
        import numpy as np
        KEEP_RATIO = 0.7
        scores = jnp.einsum('bnd,do->bn', x, w) + b[0]
        N = x.shape[1]
        k = int(round(N * KEEP_RATIO))
        _, idx = jax.lax.top_k(scores, k)
        return jnp.take_along_axis(x, idx[:, :, None], axis=1)

    def _L0_attn_ref(hidden_states, Wq, bq, Wk, bk, Wv, bv, Wo, bo, ws, bs):
        import jax, jax.numpy as jnp
        import numpy as np
        NUM_HEADS = 12

        def _shape(x, B, H, D):
            B_, S, _ = x.shape
            return x.reshape(B_, S, H, D).transpose(0, 2, 1, 3)
        B, T, E = hidden_states.shape
        H = NUM_HEADS
        D = E // H
        q = _shape(hidden_states @ Wq.T + bq, B, H, D)
        k = _shape(hidden_states @ Wk.T + bk, B, H, D)
        v = _shape(hidden_states @ Wv.T + bv, B, H, D)
        score = jnp.einsum('bhtsd,d->bhts', jnp.tanh(q[:, :, :, None, :] + k[:, :, None, :, :]), ws) + bs[0]
        p_attn = jax.nn.softmax(score, axis=-1)
        attn = jnp.einsum('bhts,bhsd->bhtd', p_attn, v)
        attn = attn.transpose(0, 2, 1, 3).reshape(B, T, E)
        return attn @ Wo.T + bo

    def _L0_ffn_ref(x, W1, b1, W2, b2, s_gelu, s_out):
        import jax, jax.numpy as jnp
        import numpy as np

        def _fq(x, scale, qmin, qmax):
            q = jnp.clip(jnp.round(x / scale), qmin, qmax) * scale
            return x + jax.lax.stop_gradient(q - x)

        def _quant_weight(W):
            scale = jnp.max(jnp.abs(W)) / 127.0
            return _fq(W, scale, -127.0, 127.0)
        h = jnp.einsum('bsd,hd->bsh', x, _quant_weight(W1)) + b1
        h = jax.nn.gelu(h, approximate=False)
        h = _fq(h, s_gelu, -128.0, 127.0)
        y = jnp.einsum('bsh,dh->bsd', h, _quant_weight(W2)) + b2
        y = _fq(y, s_out, -128.0, 127.0)
        return y

    def _L1_attn_ref(x, Wq, bq, Wk, bk, Wv, bv, Wo, bo):
        import jax, jax.numpy as jnp
        import numpy as np
        LOG2E = 1.4426950408889634
        NUM_HEADS = 12

        def fake_quant_sym8(x):
            scale = jnp.maximum(jnp.max(jnp.abs(x)) / 127.0, 1e-08)
            q = jnp.clip(jnp.round(x / scale), -128.0, 127.0) * scale
            return x + jax.lax.stop_gradient(q - x)

        def integer_approx_softmax(x):
            z = x * LOG2E
            z = z - jnp.max(z, axis=-1, keepdims=True)
            zi = jnp.floor(z)
            zf = z - zi
            p = jnp.exp2(zi) * (1.0 + zf)
            return p / jnp.sum(p, axis=-1, keepdims=True)
        B, N, E = x.shape
        H = NUM_HEADS
        D = Wq.shape[1] // H
        xq = fake_quant_sym8(x)
        Q = (xq @ Wq + bq).reshape(B, N, H, D).transpose(0, 2, 1, 3)
        K = (xq @ Wk + bk).reshape(B, N, H, D).transpose(0, 2, 1, 3)
        V = (xq @ Wv + bv).reshape(B, N, H, D).transpose(0, 2, 1, 3)
        logits = jnp.einsum('bhnd,bhmd->bhnm', Q, K)
        attn = integer_approx_softmax(logits)
        ctx = jnp.einsum('bhnm,bhmd->bhnd', attn, V)
        ctx = ctx.transpose(0, 2, 1, 3).reshape(B, N, H * D)
        return ctx @ Wo + bo

    def _L1_ffn_ref(x, W1, b1, W2, b2, Wg, bg):
        import jax, jax.numpy as jnp
        import numpy as np
        E, D, H = (16, 192, 192)
        B, N = (32, 197)
        Bx, Nx, Dx = x.shape
        t = x.reshape(-1, Dx)
        logits = t @ Wg.T + bg
        idx = jnp.argmax(logits, axis=-1)
        out = jnp.zeros_like(t)
        for e in range(W1.shape[0]):
            mask = (idx == e).astype(t.dtype)[:, None]
            h = jax.nn.gelu(t @ W1[e].T + b1[e], approximate=False)
            y = h @ W2[e].T + b2[e]
            out = out + mask * y
        return out.reshape(Bx, Nx, Dx)
    h = _L0_tok_ref(x, L0_tok_w, L0_tok_b)
    h = h + _L0_attn_ref(_layernorm(h, axis=-1), L0_attn_Wq, L0_attn_bq, L0_attn_Wk, L0_attn_bk, L0_attn_Wv, L0_attn_bv, L0_attn_Wo, L0_attn_bo, L0_attn_ws, L0_attn_bs)
    h = h + _L0_ffn_ref(_layernorm(h, axis=-1), L0_ffn_W1, L0_ffn_b1, L0_ffn_W2, L0_ffn_b2, L0_ffn_s_gelu, L0_ffn_s_out)
    h = h + _L1_attn_ref(_layernorm(h, axis=-1), L1_attn_Wq, L1_attn_bq, L1_attn_Wk, L1_attn_bk, L1_attn_Wv, L1_attn_bv, L1_attn_Wo, L1_attn_bo)
    h = h + _L1_ffn_ref(_layernorm(h, axis=-1), L1_ffn_W1, L1_ffn_b1, L1_ffn_W2, L1_ffn_b2, L1_ffn_Wg, L1_ffn_bg)
    return h

_drawn_inputs = setup_inputs


def setup_inputs(seed=0):
    import zlib

    import numpy as np

    out = dict(_drawn_inputs(seed))
    spreads = {'L1_attn_bq': (0.0, 0.8),
     'L1_attn_bk': (0.0, 2.0),
     'L1_attn_bv': (0.0, 0.316),
     'L1_attn_bo': (0.0, 0.1),
     'L1_ffn_bg': (0.0, 0.1)}
    factors = {'L0_attn_Wq': 8.0,
     'L0_attn_bq': 22.902,
     'L0_attn_Wk': 8.0,
     'L0_attn_bk': 23.196,
     'L0_attn_Wv': 4.736,
     'L0_attn_bv': 5.18,
     'L0_attn_Wo': 4.153,
     'L0_attn_ws': 8.0,
     'L0_ffn_b1': 4.579,
     'L0_ffn_b2': 5.279,
     'L1_attn_Wq': 8.0,
     'L1_attn_Wk': 8.0,
     'L1_attn_Wv': 3.458,
     'L1_ffn_b1': 23.361,
     'L1_ffn_b2': 3.353}
    for name, (base, spread) in spreads.items():
        noise = np.random.default_rng([zlib.crc32(name.encode()), seed]).standard_normal(out[name].shape)
        drawn = base * np.exp(spread * noise) if base else spread * noise
        out[name] = jnp.asarray(drawn.astype(out[name].dtype))
    for name, factor in factors.items():
        out[name] = (out[name] * factor).astype(out[name].dtype)
    return out
```

```python
from contextlib import ExitStack

import concourse.bass as bass
from concourse import mybir

F32 = mybir.dt.float32
BF16 = mybir.dt.bfloat16
I32 = mybir.dt.int32
U32 = mybir.dt.uint32
U8 = mybir.dt.uint8
ALU = mybir.AluOpType
ACT = mybir.ActivationFunctionType
AX = mybir.AxisListType
RMAX = bass.bass_isa.ReduceOp.max

B, N, D = 16, 256, 192
KEEP = int(round(N * 0.7))
TA = 128
TB = KEEP - TA
TILES = ((0, TA), (1, TB))
HEADS, HD = 12, 16
DA, DB = 128, D - 128
SLOTS = B + 2
ROWS = 2 * SLOTS

UA = KEEP
UB = (KEEP + 1) // 2
UNITS = UA + UB
UG = 16
GROUPS = -(-UNITS // UG)
BODY = 2 * GROUPS
DVE_UNITS = 10
CHUNK = 4
CHUNKS = -(-GROUPS // CHUNK)
PT_COLS = GROUPS * 128
VC = HD + 1
EPS = 1e-5
HID = 4 * D
HT = HID // 128
HW = HT * KEEP
C2 = 1.4426950408889634
ROUNDS = HEADS // 4
PAIRS = HEADS // 2
EXPERTS = 16
XT = (B * KEEP + EXPERTS * 127) // 128
MAGIC = 1.5 * 2.0 ** 23


def build(nc, I, out):
    ctx = ExitStack()
    with ctx:
        def sb(name, shape, dt=F32):
            return ctx.enter_context(nc.sbuf_tensor(name, shape, dt))

        def ps(name):
            return ctx.enter_context(nc.psum_tensor(name, [128, 512], F32))

        def sem(name):
            return ctx.enter_context(nc.semaphore(name))

        resid = sb("resid", [128, SLOTS, 2, D])
        work = sb("work", [128, 12288])
        x_all = work[:, 0:2 * B * D].rearrange("p (k d) -> p k d", d=D)
        x_prod = work[:, 2 * B * D:4 * B * D].rearrange("p (k d) -> p k d", d=D)
        cmp_junk = work[:, 2 * B * D:2 * B * D + 64].bitcast(U8)
        args = [work[:, n * UG * KEEP:(n + 1) * UG * KEEP] for n in range(2)]
        tanhs = [work[:, (n + 2) * UG * KEEP:(n + 3) * UG * KEEP] for n in range(2)]
        pt_region = sb("pt_region", [128, 9216])
        pt = [[pt_region[:, (2 * n + m) * PT_COLS:(2 * n + m + 1) * PT_COLS] for m in range(2)] for n in range(2)]
        score_rows = pt_region[:, 0:B * N]

        shared = sb("shared", [128, 4352])
        carved = [0]

        def carve(shape):
            size = 1
            for n in shape[1:]:
                size *= n
            a = shared[0:shape[0], carved[0]:carved[0] + size]
            carved[0] += size
            if len(shape) == 2:
                return a
            names = "abc"[:len(shape) - 1]
            dims = {c: n for c, n in zip(names[1:], shape[2:])}
            return a.rearrange(f"p ({' '.join(names)}) -> p {' '.join(names)}", **dims)

        ident = sb("ident", [128, 128])
        iota_keep = sb("iota_keep", [128, KEEP])
        earlier = carve([128, 2, N])
        tok_w = sb("tok_w", [128, D])
        tok_b = sb("tok_b", [128, 1])
        ws_col = sb("ws_col", [128, 1])
        bs_neg = sb("bs_neg", [128, 1])
        ws_place = sb("ws_place", [128, 4, 32])
        wq0 = [carve([DA, 256]), carve([DB + 1, 256])]
        wk0 = [carve([DA, 256]), carve([DB + 1, 256])]
        wv0 = [sb("wv0a", [DA, D]), sb("wv0b", [DB + 1, D])]
        wo0 = [sb("wo0a", [DA, D]), sb("wo0b", [DB + 1, D])]

        tok_score = sb("tok_score", [128, 2 * B])
        tok_rowsT = sb("tok_rowsT", [2 * B, 128])
        above = sb("above", [128, 2 * B])
        ties = sb("ties", [128, 2 * B])
        rank = sb("rank", [128, 2 * B])
        onehot = carve([128, 2, 2, KEEP])
        stats = sb("stats", [128, ROWS, 6])
        mean = sb("mean", [128, ROWS])
        diff = sb("diff", [128, ROWS])
        var = sb("var", [128, ROWS])
        std = sb("std", [128, ROWS])
        rstd = sb("rstd", [128, ROWS])
        newt = sb("newt", [128, ROWS])
        normed = sb("normed", [128, 2, D])
        xT = [sb("xTa", [DA, KEEP]), sb("xTb", [DB + 1, KEEP])]
        q_cols = [carve([128, UNITS + 1]) for n in range(2)]
        k_sb = [carve([128, 2 * KEEP]) for n in range(2)]
        v_sb = [carve([128, 2, HEADS, VC]) for n in range(2)]
        s_sb = [sb(f"s_sb{n}", [128, KEEP]) for n in range(2)]
        s_min = [sb(f"s_min{n}", [128, 1]) for n in range(2)]
        p_sb = [sb(f"p_sb{n}", [128, KEEP]) for n in range(2)]
        inv_sum = sb("inv_sum", [128, 2, HEADS])
        ctx_sb = sb("ctx_sb", [128, 2, D])
        ctxT = [sb("ctxTa", [DA, KEEP]), sb("ctxTb", [DB + 1, KEEP])]

        w1q = [sb("w1qa", [DA, HID]), sb("w1qb", [DB, HID])]
        w2f = sb("w2f", [128, HT, D])
        w2q = sb("w2q", [128, HT, D], BF16)
        b1_col = sb("b1_col", [128, HT])
        b2_row = sb("b2_row", [128, D])
        s_gelu = sb("s_gelu", [128, 1])
        s_out = sb("s_out", [128, 1])
        w_max = sb("w_max", [128, 3])
        w_maxes = sb("w_maxes", [128, 2])
        w_all = sb("w_all", [128, 2])
        w_scale = sb("w_scale", [128, 2])
        w_inv = sb("w_inv", [128, 2])
        inv_gelu = sb("inv_gelu", [128, 1])
        inv_out = sb("inv_out", [128, 1])
        y_scale = sb("y_scale", [128, 1])
        fx = [[sb(f"fx{n}a", [DA, KEEP]), sb(f"fx{n}b", [DB, KEEP])] for n in range(2)]
        fnorm = [normed, sb("fnorm1", [128, 2, D])]
        gelu = [pt_region[:, n * HW:(n + 1) * HW] for n in range(2)]
        hq = [pt_region[:, 2 * HW + n * HW // 2:2 * HW + (n + 1) * HW // 2].bitcast(BF16) for n in range(2)]
        y_sb = sb("y_sb", [128, 2, D])

        psum = ctx.enter_context(nc.psum_tensor("psum", [128, 8 * 512], F32))
        bank_k0, bank_k1, bank_s0, bank_s1, bank_pta, bank_ptb, bank_pre, bank_out = (
            psum[:, 512 * n:512 * n + 512] for n in range(8))
        bank_k, bank_s, bank_pt = [bank_k0, bank_k1], [bank_s0, bank_s1], [bank_pta, bank_ptb]
        pair_banks = [psum[:, 1024 * n:1024 * n + 1024].rearrange("p (e c) -> p e c", e=2)[:, :, 0:2 * KEEP]
                      .rearrange("p e (t s) -> p e t s", t=2) for n in range(2)]

        xn3 = work[:, 0:2 * B * D].rearrange("p (k d) -> p k d", d=D)
        y1 = [work[:, 2 * B * D + n * 4 * KEEP:2 * B * D + (n + 1) * 4 * KEEP] for n in range(2)]
        p1 = [work[:, 2 * B * D + (n + 2) * 4 * KEEP:2 * B * D + (n + 3) * 4 * KEEP] for n in range(2)]
        ctx1 = work[:, 2 * B * D + 16 * KEEP:2 * B * D + 19 * KEEP]
        PT1 = HEADS * KEEP
        pt1 = [[pt_region[:, (2 * n + m) * PT1:(2 * n + m + 1) * PT1] for m in range(2)] for n in range(2)]
        ew1 = [work[:, 0:EXPERTS * D], work[0:DB + 1, EXPERTS * D:2 * EXPERTS * D]]
        ew2 = [work[:, 2 * EXPERTS * D:3 * EXPERTS * D], work[0:DB + 1, 3 * EXPERTS * D:4 * EXPERTS * D]]
        xn4 = pt_region[:, 0:2 * B * D].rearrange("p (k d) -> p k d", d=D)
        KE = 2 * B * EXPERTS
        wg = [sb("wga", [DA, EXPERTS]), sb("wgb", [DB + 1, EXPERTS])]
        carved[0] = 0
        gxT = [[carve([DA, KEEP]), carve([DB + 1, KEEP])] for n in range(2)]
        lower = carve([128, 128])
        ones = carve([128, 128])
        valid = sb("valid", [128, 2 * B])
        iota_e = sb("iota_e", [128, EXPERTS])
        iota_t = sb("iota_t", [128, XT])
        carry = carve([128, EXPERTS, 2 * B])
        gate = [pt_region[:, 2 * B * D + n * KE:2 * B * D + (n + 1) * KE].rearrange("p (e k) -> p e k", e=EXPERTS)
                for n in range(4)]
        top = sb("top", [128, 2 * B])
        counts = sb("counts", [128, EXPERTS])
        counts_i = sb("counts_i", [128, EXPERTS], I32)
        tiles_f = sb("tiles_f", [128, EXPERTS])
        ends = sb("ends", [128, EXPERTS])
        base = sb("base", [128, EXPERTS])
        ended = carve([128, XT, EXPERTS])
        owner = sb("owner", [128, XT])
        owner_i = sb("owner_i", [128, XT], I32)
        slot_f = sb("slot_f", [128, 2 * B])
        slot_i = sb("slot_i", [128, 2 * B], U32)
        zeros = sb("zeros", [128, D])
        xs = [carve([128, D]) for n in range(2)]
        exT = [[carve([DA, 128]), carve([DB + 1, 128])] for n in range(2)]
        eh = [carve([128, D]) for n in range(2)]
        ehT = [[carve([DA, 128]), carve([DB + 1, 128])] for n in range(2)]
        ey = [carve([128, D]) for n in range(2)]
        xs_dram = nc.dram_tensor("xs_dram", (XT * 128, D), F32, kind="Internal").ap()
        ys_dram = nc.dram_tensor("ys_dram", (XT * 128, D), F32, kind="Internal").ap()
        ident16 = sb("ident16", [128, 128], BF16)
        wsrc = [[sb(f"wsrc{n}a", [DA, D]), sb(f"wsrc{n}b", [DB, D])] for n in range(3)]
        wrest = sb("wrest", [128, D])
        w1parts = [[[sb(f"w1p{n}{m}{r}", [rows, HEADS * (32 if n < 2 else HD)], BF16) for r, rows in enumerate((DA, DB))]
                    for m in range(3)] for n in range(3)]
        wo1 = [sb("wo1a", [DA, D]), sb("wo1b", [DB + 1, D])]
        bqk1 = [sb(f"bqk1{n}", [128, ROUNDS]) for n in range(2)]
        bv1 = sb("bv1", [128, D])
        mx3 = sb("mx3", [128, 2 * B])
        x_max = sb("x_max", [128, 1])
        x_allmax = sb("x_allmax", [128, 1])
        x_scale = sb("x_scale", [128, 1])
        x_inv = sb("x_inv", [128, 1])
        xq = [sb(f"xq{n}", [128, 2, D], BF16) for n in range(2)]
        xqT = [[sb(f"xqT{n}a", [DA, KEEP], BF16), sb(f"xqT{n}b", [DB, KEEP], BF16)] for n in range(2)]
        carved[0] = 0
        q1 = [carve([128, ROUNDS, 2 * TA]) for n in range(2)]
        k1 = [carve([128, ROUNDS, KEEP]) for n in range(2)]
        v1 = [carve([128, 2, HEADS, 32]) for n in range(2)]
        pmax = [sb(f"pmax{n}", [128, 2, 2]) for n in range(2)]
        pneg = [sb(f"pneg{n}", [128, 4]) for n in range(2)]

        out_banks = [bank_pre, bank_out]
        ffn_banks = [[bank_k[0], bank_k[1], bank_s[0]], [bank_s[1], bank_pt[0], bank_pt[1]]]

        scores_dram = nc.dram_tensor("scores_dram", (2 * B, 128), F32, kind="Internal").ap()

        x_loaded = sem("x_loaded")
        small_loaded = sem("small_loaded")
        w0_loaded = sem("w0_loaded")
        consts = sem("consts")
        const_step = sem("const_step")
        ws_ready = sem("ws_ready")
        dots_done = sem("dots_done")
        scores_ready = sem("scores_ready")
        scoresT_psum = sem("scoresT_psum")
        scoresT_ready = sem("scoresT_ready")
        scores_stored = sem("scores_stored")
        rows_loaded = sem("rows_loaded")
        compared = sem("compared")
        rank_ready = sem("rank_ready")
        onehot_ready = sem("onehot_ready")
        picked = sem("picked")
        resid_ready = sem("resid_ready")
        filled = sem("filled")
        stats_done = sem("stats_done")
        ln_step = sem("ln_step")
        var_ready = sem("var_ready")
        std_ready = sem("std_ready")
        ln_ready = sem("ln_ready")

        normed_ready = sem("normed_ready")
        xT_psum = sem("xT_psum")
        xT_ready = sem("xT_ready")
        q_psum = sem("q_psum")
        k_psum = sem("k_psum")
        q_ready = sem("q_ready")
        k_ready = sem("k_ready")
        v_psum = sem("v_psum")
        v_ready = sem("v_ready")
        args_dve = sem("args_dve")
        args_pool = sem("args_pool")
        tanh_done = sem("tanh_done")
        scored = sem("scored")
        smax_done = sem("smax_done")
        exp_done = sem("exp_done")
        turned = sem("turned")
        pt_ready = sem("pt_ready")
        ctx_psum = sem("ctx_psum")
        ctx_inv = sem("ctx_inv")
        ctx_ready = sem("ctx_ready")
        ctxT_psum = sem("ctxT_psum")
        ctxT_ready = sem("ctxT_ready")
        proj_psum = sem("proj_psum")
        resid_added = sem("resid_added")
        stored = sem("stored")

        wf_loaded = sem("wf_loaded")
        w_step = sem("w_step")
        w_maxed = sem("w_maxed")
        w_alled = sem("w_alled")
        f_normed = sem("f_normed")
        f_xT_psum = sem("f_xT_psum")
        f_xT_ready = sem("f_xT_ready")
        h_psum = sem("h_psum")
        gelu_done = sem("gelu_done")
        quant_step = sem("quant_step")
        hq_ready = sem("hq_ready")
        y_psum = sem("y_psum")
        y_step = sem("y_step")
        f_added = sem("f_added")
        w1_loaded = sem("w1_loaded")
        w1_step = sem("w1_step")
        w1_ready = sem("w1_ready")
        qv_blank = sem("qv_blank")
        n3_step = sem("n3_step")
        x_maxed = sem("x_maxed")
        x_alled = sem("x_alled")
        x3_step = sem("x3_step")
        xq_ready = sem("xq_ready")
        xqT_psum = sem("xqT_psum")
        xqT_ready = sem("xqT_ready")
        qkv_psum = sem("qkv_psum")
        qkv_out = sem("qkv_out")
        pair_scored = sem("pair_scored")
        pair_maxed = sem("pair_maxed")
        pair_neg = sem("pair_neg")
        pair_scaled = sem("pair_scaled")
        pair_clipped = sem("pair_clipped")
        pair_powered = sem("pair_powered")
        pair_turned = sem("pair_turned")
        pair_pt = sem("pair_pt")
        ctx1_psum = sem("ctx1_psum")
        ctx1_out = sem("ctx1_out")
        ctx1_tokens = sem("ctx1_tokens")
        ctx1_inv = sem("ctx1_inv")
        ctx1_ready = sem("ctx1_ready")
        ctx1T_psum = sem("ctx1T_psum")
        ctx1T_ready = sem("ctx1T_ready")
        proj1_psum = sem("proj1_psum")
        added1 = sem("added1")
        e_consts = sem("e_consts")
        e_zeroed = sem("e_zeroed")
        e_loaded = sem("e_loaded")
        n4_ready = sem("n4_ready")
        gxT_psum = sem("gxT_psum")
        gxT_ready = sem("gxT_ready")
        gate_psum = sem("gate_psum")
        gate_out = sem("gate_out")
        g_step = sem("g_step")
        chosen = sem("chosen")
        prefix_psum = sem("prefix_psum")
        slots_ready = sem("slots_ready")
        sent = sem("sent")
        xs_loaded = [sem(f"xs_loaded{n}") for n in range(2)]
        exT_psum = sem("exT_psum")
        exT_ready = sem("exT_ready")
        eh_psum = sem("eh_psum")
        eh_ready = sem("eh_ready")
        ehT_psum = sem("ehT_psum")
        ehT_ready = sem("ehT_ready")
        ey_psum = sem("ey_psum")
        ey_ready = sem("ey_ready")
        ys_stored = [sem(f"ys_stored{n}") for n in range(2)]
        back = [sem(f"back{n}") for n in range(4)]
        summed = sem("summed")

        block = ctx.enter_context(nc.Block())

        def units(g):
            return min(UG, UNITS - g * UG)

        def parts(g, lo, hi):
            hi = min(hi, units(g))
            cut = min(max(UA - g * UG, lo), hi)
            return [(h, a, e) for h, a, e in ((0, lo, cut), (1, cut, hi)) if e > a]

        def sums(eng, dst, k, q, g, lo, hi):
            for h, a, e in parts(g, lo, hi):
                ins = eng.tensor_tensor(
                    dst[:, a * KEEP:e * KEEP].rearrange("p (u s) -> p u s", s=KEEP),
                    k[:, h * KEEP:(h + 1) * KEEP].unsqueeze(1).to_broadcast([128, e - a, KEEP]),
                    q[:, g * UG + a:g * UG + e].unsqueeze(2).to_broadcast([128, e - a, KEEP]), ALU.add)
            return ins

        def staged(eng, step, lags, count=B):
            ahead, behind = lags
            first = max(4, behind + behind % 2)
            last = count - ahead - (count - ahead) % 2
            for i in range(first):
                step(i, i % 2)
            with eng.Fori(first // 2, last // 2) as j:
                for par in range(2):
                    step(2 * j + par, par)
            for i in range(last, count + behind):
                step(i, i % 2)

        def real(b, count=B):
            return not isinstance(b, int) or 0 <= b < count

        def need(eng, sem, value):
            if not isinstance(value, int) or value > 0:
                eng.wait_ge(sem, value)

        @block.sync
        def _(sp):
            xv = I["x"].rearrange("b (t p) d -> p (b t) d", p=128)
            for n in range(4):
                sp.dma_start(x_all[:, 8 * n:8 * n + 8, :], xv[:, 8 * n:8 * n + 8, :]).then_inc(x_loaded, 16)
            sp.wait_ge(scoresT_ready, 1)
            sp.dma_start(scores_dram, tok_rowsT[:, :]).then_inc(scores_stored, 16)
            sp.wait_ge(scores_stored, 16)
            flat = scores_dram.rearrange("k p -> (k p)")
            for n in range(4):
                cols = slice(n * B * N // 4, (n + 1) * B * N // 4)
                sp.dma_start(score_rows[:, cols], flat[cols].partition_broadcast(128)).then_inc(rows_loaded, 16)
            for r, (lo, hi) in enumerate(((0, DA), (DA, D))):
                sp.dma_start(w1q[r][:, :], I["L0_ffn_W1T"][lo:hi, :]).then_inc(wf_loaded, 16)
            sp.dma_start(w2f[:, :, :], I["L0_ffn_W2T"].rearrange("(c p) d -> p c d", p=128)).then_inc(wf_loaded, 16)
            sp.dma_start(b1_col[:, :], I["L0_ffn_b1_cols"]).then_inc(wf_loaded, 16)
            sp.dma_start(b2_row[:, :], I["L0_ffn_b2"].partition_broadcast(128)).then_inc(wf_loaded, 16)
            sp.dma_start(s_gelu[:, :], I["L0_ffn_s_gelu"].partition_broadcast(128)).then_inc(wf_loaded, 16)
            sp.dma_start(s_out[:, :], I["L0_ffn_s_out"].partition_broadcast(128)).then_inc(wf_loaded, 16)
            for n, name in enumerate("qkv"):
                for r, (lo, hi) in enumerate(((0, DA), (DA, D))):
                    sp.dma_start(wsrc[n][r][:, :], I[f"L1_attn_W{name}"][lo:hi, :]).then_inc(w1_loaded, 16)
            sp.dma_start(bv1[:, :], I["L1_attn_bv"].partition_broadcast(128)).then_inc(w1_loaded, 16)
            for r, (lo, hi) in enumerate(((0, DA), (DA, D))):
                sp.dma_start(wo1[r][0:hi - lo, :], I["L1_attn_Wo"][lo:hi, :]).then_inc(w1_loaded, 16)
            sp.dma_start(wo1[1][DB:DB + 1, :], I["L1_attn_bo"].rearrange("(o d) -> o d", o=1)).then_inc(w1_loaded, 16)
            sp.wait_ge(w1_step, 2)
            for j in range(4):
                for n, name in enumerate("qk"):
                    sp.dma_start(bqk1[n][32 * j:32 * j + HD, :],
                                 I[f"L1_attn_b{name}_cols"][HD * j:HD * j + HD, :]).then_inc(w1_loaded, 16)
            sp.wait_ge(e_consts, 1)
            sp.dma_start(xs_dram.rearrange("(j p) d -> p j d", p=128),
                         zeros[:, :].unsqueeze(1).to_broadcast([128, XT, D])).then_inc(e_zeroed, 16)
            for r, (lo, hi) in enumerate(((0, DA), (DA, D))):
                sp.dma_start(wg[r][0:hi - lo, :], I["L1_ffn_WgT"][lo:hi, :]).then_inc(e_loaded, 16)
            sp.dma_start(wg[1][DB:DB + 1, :], I["L1_ffn_bg"].rearrange("(o d) -> o d", o=1)).then_inc(e_loaded, 16)
            sp.wait_ge(added1, 2 * B)
            for dst, wt, bias in ((ew1, "L1_ffn_W1T", "L1_ffn_b1"), (ew2, "L1_ffn_W2T", "L1_ffn_b2")):
                for r, (lo, hi) in enumerate(((0, DA), (DA, D))):
                    sp.dma_start(dst[r][0:hi - lo, :].rearrange("p (e h) -> p e h", h=D),
                                 I[wt][:, lo:hi, :].rearrange("e p h -> p e h")).then_inc(e_loaded, 16)
                sp.dma_start(dst[1][DB:DB + 1, :], I[bias].rearrange("(o e) d -> o (e d)", o=1)).then_inc(e_loaded, 16)

            sp.wait_ge(sent, 16 * 2 * B)

            def expert_step(i, par):
                if real(i, XT):
                    need(sp, exT_psum, i - 1)
                    sp.dma_start(xs[par][:, :], xs_dram[bass.ds(128 * i, 128), :]).then_inc(xs_loaded[par], 16)
                if real(i - 4, XT):
                    sp.wait_ge(ey_ready, i - 3)
                    sp.dma_start(ys_dram[bass.ds(128 * (i - 4), 128), :], ey[par][:, :]).then_inc(ys_stored[par], 16)

            staged(sp, expert_step, (0, 4), XT)
            for b in range(B):
                sp.wait_ge(summed, b + 1)
                for t, rows in TILES:
                    sp.dma_start(out[b, t * TA:t * TA + rows, :], resid[0:rows, b + 1, t, :]).then_inc(stored, 16)
            sp.wait_ge(stored, 16 * 2 * B)

        @block.gpsimd
        def _(pool):
            step = [0]

            def chain(ins):
                step[0] += 1
                ins.then_inc(const_step, 1)
                pool.wait_ge(const_step, step[0])

            chain(pool.memset(ident[:, :], 0.0))
            chain(pool.affine_select(out=ident[:, :], in_=ident[:, :], compare_op=ALU.not_equal, fill=1.0,
                                     base=0, pattern=[[-1, 128]], channel_multiplier=1))
            pool.iota(iota_keep[:, :], pattern=[[1, KEEP]], base=0, channel_multiplier=0,
                      allow_small_or_imprecise_dtypes=True)
            chain(pool.memset(earlier[:, :, :], 1.0))
            chain(pool.affine_select(out=earlier[:, :, :], in_=earlier[:, :, :], compare_op=ALU.is_gt, fill=0.0,
                                     base=0, pattern=[[128, 2], [-1, N]], channel_multiplier=1))
            chain(pool.memset(ws_place[:, :, :], 1.0))
            chain(pool.affine_select(out=ws_place[:, :, :], in_=ws_place[:, :, :], compare_op=ALU.is_ge, fill=0.0,
                                     base=0, pattern=[[8 * HD, 4], [-HD, 32]], channel_multiplier=1))
            pool.affine_select(out=ws_place[:, :, :], in_=ws_place[:, :, :], compare_op=ALU.is_ge, fill=0.0,
                               base=HD - 1, pattern=[[-8 * HD, 4], [HD, 32]],
                               channel_multiplier=-1).then_inc(consts, 1)

            for n in range(2):
                pool.memset(bqk1[n][:, :], 0.0).then_inc(w1_step, 1)
            pool.tensor_copy(ident16[:, :], ident[:, :])
            for n in range(2):
                for m in range(3):
                    for r in range(2):
                        pool.memset(w1parts[n][m][r][:, :], 0.0)
            pool.memset(mx3[:, :], 0.0).then_inc(w1_step, 1)

            pool.memset(zeros[:, :], 0.0).then_inc(e_consts, 1)
            pool.wait_ge(w_maxed, 1)
            pool.partition_all_reduce(w_all[:, :], w_maxes[:, :], 128, RMAX).then_inc(w_alled, 1)

            def pool_sums(b, par, g):
                n = b * GROUPS + g
                if g == 0:
                    pool.wait_ge(q_ready, b + 1)
                    pool.wait_ge(k_ready, b + 1)
                pool.wait_ge(tanh_done, n + 1)
                sums(pool, args[(par * GROUPS + g) % 2], k_sb[par], q_cols[par], g, DVE_UNITS, UG).then_inc(args_pool, 1)

            pool.wait_ge(picked, B + 2)
            with pool.Fori(0, B // 2) as i:
                for par in range(2):
                    for g in range(GROUPS):
                        pool_sums(2 * i + par, par, g)

            pool.wait_ge(w1_loaded, 16 * 18)
            pool.wait_ge(w1_step, 3)
            at = [3]

            def chain1(ins):
                at[0] += 1
                ins.then_inc(w1_step, 1)
                pool.wait_ge(w1_step, at[0])

            for n in range(3):
                for r, rows in enumerate((DA, DB)):
                    src = wsrc[n][r][:, :].rearrange("p (h d) -> p h d", d=HD)
                    rest = wrest[0:rows, :].rearrange("p (h d) -> p h d", d=HD)
                    for m in range(3):
                        part = w1parts[n][m][r][:, :].rearrange("p (h c) -> p h c", h=HEADS)[:, :, 0:HD]
                        chain1(pool.tensor_copy(part, src))
                        if m < 2:
                            chain1(pool.tensor_tensor(rest, src, part, ALU.subtract))
                            src = rest
            pool.sem_inc(w1_ready, 1)
            pool.wait_ge(args_pool, B * GROUPS)
            pool.wait_ge(resid_added, 2 * (B + 1))
            for n in range(2):
                pool.memset(q1[n][:, :, :], 0.0)
                pool.memset(v1[n][:, :, :, :], 0.0).then_inc(qv_blank, 1)
            pool.wait_ge(qv_blank, 2)
            for n in range(2):
                pool.memset(v1[n][:, :, :, HD:HD + 1], 1.0).then_inc(qv_blank, 1)

            pool.wait_ge(x_maxed, 1)
            pool.partition_all_reduce(x_allmax[:, :], x_max[:, :], 128, RMAX).then_inc(x_alled, 1)
            pool.wait_ge(added1, 2 * B)
            pool.memset(lower[:, :], 1.0)
            pool.memset(ones[:, :], 1.0)
            pool.memset(valid[:, :], 1.0)
            pool.memset(carry[:, :, :], 1.0)
            pool.iota(iota_e[:, :], pattern=[[1, EXPERTS]], base=-EXPERTS, channel_multiplier=0,
                      allow_small_or_imprecise_dtypes=True)
            pool.iota(iota_t[:, :], pattern=[[1, XT]], base=0, channel_multiplier=0,
                      allow_small_or_imprecise_dtypes=True).then_inc(e_consts, 1)
            pool.wait_ge(e_consts, 2)
            pool.affine_select(out=lower[:, :], in_=lower[:, :], compare_op=ALU.is_gt, fill=0.0,
                               base=0, pattern=[[1, 128]], channel_multiplier=-1)
            pool.affine_select(out=valid[:, 1::2], in_=valid[:, 1::2], compare_op=ALU.is_ge, fill=0.0,
                               base=TB - 1, pattern=[[0, B]], channel_multiplier=-1)
            pool.memset(carry[:, :, 0:1], 0.0).then_inc(e_consts, 1)
            pool.wait_ge(e_consts, 3)
            for turned_x in (gxT, exT, ehT):
                for n in range(2):
                    ins = pool.memset(turned_x[n][1][DB:DB + 1, :], 1.0)
            ins.then_inc(e_consts, 1)

            pool.wait_ge(slots_ready, 1)
            pool.wait_ge(e_zeroed, 16)
            for k in range(2 * B):
                rows = TILES[k % 2][1]
                pool.indirect_dma_start(xs_dram[:, :], bass.IndirectOffsetOnAxis(ap=slot_i[0:rows, k:k + 1], axis=0),
                                        xn4[0:rows, k, :], None).then_inc(sent, 16)
            pool.wait_ge(sent, 16 * 2 * B)
            for n in range(2):
                pool.wait_ge(ys_stored[n], 8 * XT)
            for k in range(2 * B):
                rows = TILES[k % 2][1]
                need(pool, summed, k // 2 - 3)
                pool.indirect_dma_start(xn4[0:rows, k, :], None, ys_dram[:, :],
                                        bass.IndirectOffsetOnAxis(ap=slot_i[0:rows, k:k + 1], axis=0)).then_inc(back[k // 2 % 4], 16)


        @block.scalar
        def _(act):
            sd = small_loaded
            act.dma_start(tok_w[:, :], I["L0_tok_w"].rearrange("d o -> (d o)").partition_broadcast(128)).then_inc(sd, 16)
            act.dma_start(tok_b[:, :], I["L0_tok_b"].partition_broadcast(128)).then_inc(sd, 16)
            act.dma_start(bs_neg[:, :], I["L0_attn_bs"].partition_broadcast(128)).then_inc(sd, 16)
            for h in range(8):
                act.dma_start(ws_col[HD * h:HD * h + HD, :], I["L0_attn_ws"].rearrange("(d o) -> d o", o=1)).then_inc(sd, 16)
            w = w0_loaded
            for dst, wt, bias in ((wq0, "L0_attn_WqT", "L0_attn_bq"), (wk0, "L0_attn_WkT", "L0_attn_bk")):
                for r, (lo, hi) in enumerate(((0, DA), (DA, D))):
                    act.dma_start(dst[r][0:hi - lo, 0:D], I[wt][lo:hi, :]).then_inc(w, 16)
                    act.dma_start(dst[r][0:hi - lo, D:256], I[wt][lo:hi, DA:D]).then_inc(w, 16)
                row = I[bias].rearrange("(o d) -> o d", o=1)
                act.dma_start(dst[1][DB:DB + 1, 0:D], row).then_inc(w, 16)
                act.dma_start(dst[1][DB:DB + 1, D:256], row[:, DA:D]).then_inc(w, 16)
            for dst, wt, bias in ((wv0, "L0_attn_WvT", "L0_attn_bv"), (wo0, "L0_attn_WoT", "L0_attn_bo")):
                act.dma_start(dst[0][:, :], I[wt][0:DA, :]).then_inc(w, 16)
                act.dma_start(dst[1][0:DB, :], I[wt][DA:D, :]).then_inc(w, 16)
                act.dma_start(dst[1][DB:DB + 1, :], I[bias].rearrange("(o d) -> o d", o=1)).then_inc(w, 16)

            act.wait_ge(filled, 1)
            act.sem_inc(resid_ready, 2)
            with act.Fori(0, B // 2) as i:
                for par in range(2):
                    b = 2 * i + par
                    act.wait_ge(picked, b + 3)
                    for t, rows in TILES:
                        ins = act.activation(resid[0:rows, b + 1, t, :], bank_k[par][0:rows, t * D:(t + 1) * D], ACT.Copy)
                    ins.then_inc(resid_ready, 1)
            act.wait_ge(var_ready, 1)
            act.activation(std[:, :], var[:, :], ACT.Sqrt).then_inc(std_ready, 1)

            act.preload_act_table_set("exp_and_others")
            act.sem_inc(tanh_done, 2)
            act.sem_inc(exp_done, 2)

            def exps(n, slot):
                act.wait_ge(smax_done, n + 1)
                act.wait_ge(turned, n + 1)
                act.activation(p_sb[slot][:, :], s_sb[slot][:, :], ACT.Exp, bias=s_min[slot][:, :],
                               scale=-1.0).then_inc(exp_done, 1)

            with act.Fori(0, B // 2) as i:
                for par in range(2):
                    for g in range(GROUPS):
                        n = i * BODY + par * GROUPS + g
                        slot = (par * GROUPS + g) % 2
                        act.wait_ge(args_dve, n + 1)
                        act.wait_ge(args_pool, n + 1)
                        act.wait_ge(scored, n + 1)
                        w = units(g) * KEEP
                        act.activation(tanhs[slot][:, 0:w], args[slot][:, 0:w], ACT.Tanh).then_inc(tanh_done, 1)
                        exps(n, slot)
            for n in range(B * GROUPS, B * GROUPS + 2):
                exps(n, n % 2)

            act.wait_ge(var_ready, 2)
            act.activation(std[:, :], var[:, :], ACT.Sqrt).then_inc(std_ready, 1)
            act.preload_act_table(ACT.Gelu)

            def ffn_step(i, par):
                if real(i + 1):
                    act.wait_ge(f_xT_psum, i + 2)
                    if not isinstance(i, int) or i >= 1:
                        act.wait_ge(h_psum, HT // 2 * i)
                    x = fx[1 - par]
                    act.activation(x[0][:, :], bank_pre[:, 0:KEEP], ACT.Copy)
                    act.activation(x[1][:, :], bank_pre[0:DB, KEEP:2 * KEEP], ACT.Copy).then_inc(f_xT_ready, 1)
                if real(i):
                    if not isinstance(i, int) or i >= 2:
                        act.wait_ge(hq_ready, i - 1)
                    for c in range(HT):
                        if c % 2 == 0:
                            act.wait_ge(h_psum, HT // 2 * i + c // 2 + 1)
                        ins = act.activation(gelu[par][:, c * KEEP:(c + 1) * KEEP],
                                             ffn_banks[par][c // 2][:, c % 2 * KEEP:(c % 2 + 1) * KEEP],
                                             ACT.Gelu, bias=b1_col[:, c:c + 1], scale=w_scale[:, 0:1])
                    ins.then_inc(gelu_done, 1)

            ffn_step(-1, 1)
            staged(act, ffn_step, (1, 0))

            act.wait_ge(var_ready, 3)
            act.activation(std[:, :], var[:, :], ACT.Sqrt).then_inc(std_ready, 1)
            act.preload_act_table_set("exp_and_others")

            def attn1_step(b, par):
                for u in range(PAIRS):
                    n, slot = PAIRS * b + u, u % 2
                    m = n - 2
                    if real(m, PAIRS * B):
                        uu, pp = ((u - 2), par) if u >= 2 else (u - 2 + PAIRS, 1 - par)
                        act.wait_ge(pair_turned, m + 1)
                        cols = slice(2 * uu * KEEP, 2 * uu * KEEP + 2 * KEEP)
                        act.activation(pt1[pp][0][:, cols], bank_pt[0][:, 0:2 * KEEP], ACT.Copy)
                        act.activation(pt1[pp][1][0:TB, cols], bank_pt[1][0:TB, 0:2 * KEEP], ACT.Copy).then_inc(pair_pt, 1)
                    if real(n, PAIRS * B):
                        act.wait_ge(pair_neg, n + 1)
                        need(act, pair_clipped, n - 1)
                        for e in range(2):
                            for t in range(2):
                                c = 2 * e + t
                                ins = act.activation(y1[slot][:, c * KEEP:(c + 1) * KEEP], pair_banks[slot][:, e, t, :],
                                                     ACT.Identity, bias=pneg[slot][:, c:c + 1], scale=C2 * 2.0 ** 23)
                        ins.then_inc(pair_scaled, 1)
                    if u == 0 and real(b - 1):
                        ctx1_part(b - 1, 0, 2, 0)
                    if u == 2 and real(b - 1):
                        ctx1_part(b - 1, 2, 3, 1)
                    if u == 4 and real(b - 1):
                        act.wait_ge(ctx1T_psum, b)
                        act.activation(ctxT[0][:, :], bank_out[:, 0:KEEP], ACT.Copy)
                        act.activation(ctxT[1][0:DB, :], bank_out[0:DB, KEEP:2 * KEEP], ACT.Copy).then_inc(ctx1T_ready, 1)
                    if u == 1 and real(b + 1):
                        xqT_out(b + 1, 1 - par)
                    if u == 3 and real(b + 1):
                        k_out(b + 1, 1 - par)

            def ctx1_part(b, lo, hi, k):
                act.wait_ge(ctx1_psum, 2 * b + k + 1)
                act.activation(ctx1[:, lo * KEEP:hi * KEEP], bank_out[:, 0:(hi - lo) * KEEP], ACT.Copy).then_inc(ctx1_out, 1)

            def xqT_out(c, par):
                act.wait_ge(xqT_psum, c + 1)
                b16 = bank_pre.bitcast(BF16)
                act.activation(xqT[par][0][:, :], b16[:, 0:KEEP], ACT.Copy)
                act.activation(xqT[par][1][:, :], b16[0:DB, 256:256 + KEEP], ACT.Copy).then_inc(xqT_ready, 1)

            def k_out(c, par):
                act.wait_ge(qkv_psum, 4 * c + 2)
                for r in range(2):
                    ins = act.activation(k1[par][:, r, :], bank_pre[:, r * KEEP:(r + 1) * KEEP],
                                         ACT.Identity, bias=bqk1[1][:, r:r + 1], scale=x_scale[:, :])
                ins.then_inc(qkv_out, 1)

            act.wait_ge(x3_step, 2)
            xqT_out(0, 0)
            k_out(0, 0)
            staged(act, attn1_step, (1, 1))

            act.wait_ge(var_ready, 4)
            act.activation(std[:, :], var[:, :], ACT.Sqrt).then_inc(std_ready, 1)
            act.preload_act_table(ACT.Gelu)
            act.wait_ge(e_consts, 4)

            def gate_step(i, par):
                act.wait_ge(gxT_psum, i + 1)
                need(act, gate_psum, i - 1)
                act.activation(gxT[par][0][:, :], bank_k[par][:, 0:KEEP], ACT.Copy)
                act.activation(gxT[par][1][0:DB, :], bank_k[par][0:DB, KEEP:2 * KEEP], ACT.Copy).then_inc(gxT_ready, 1)

            staged(act, gate_step, (0, 0))

            def expert_step(i, par):
                if real(i - 1, XT):
                    act.wait_ge(eh_psum, i)
                    need(act, ehT_psum, i - 2)
                    act.activation(eh[1 - par][:, :], bank_s[1 - par][:, 0:D], ACT.Gelu).then_inc(eh_ready, 1)
                if real(i - 3, XT):
                    act.wait_ge(ey_psum, i - 2)
                    if real(i - 5, XT):
                        act.wait_ge(ys_stored[1 - par], 8 * (i - 6 + par) + 16)
                    act.activation(ey[1 - par][:, :], out_banks[1 - par][:, 0:D], ACT.Copy).then_inc(ey_ready, 1)

            staged(act, expert_step, (0, 5), XT)

        @block.vector
        def _(dve):
            for part in (resid[:, 0, :, :], resid[:, SLOTS - 1, :, :], stats[:, :, :], mean[:, :], rstd[:, :],
                         q_cols[0][:, :], q_cols[1][:, :], v_sb[0][:, :, :, :], v_sb[1][:, :, :, :],
                         xT[1][DB:DB + 1, :], ctxT[1][DB:DB + 1, :],
                         bank_s[0][:, :], bank_s[1][:, :], bank_pt[0][:, :], bank_pt[1][:, :], p_sb[0][:, :], p_sb[1][:, :]):
                ins = dve.memset(part, 1.0)
            ins.then_inc(filled, 1)
            dve.wait_ge(filled, 1)

            dve.wait_ge(small_loaded, 16 * 11)
            dve.wait_ge(x_loaded, 16 * 4)
            for k in range(2 * B):
                ins = dve.tensor_tensor_reduce(x_prod[:, k, :], x_all[:, k, :], tok_w[:, :], 1.0, 0.0,
                                               ALU.mult, ALU.add, tok_score[:, k:k + 1])
            ins.then_inc(dots_done, 1)
            dve.wait_ge(dots_done, 1)
            dve.tensor_scalar(tok_score[:, :], tok_score[:, :], tok_b[:, :], None, ALU.add).then_inc(scores_ready, 1)
            dve.wait_ge(consts, 1)
            dve.tensor_scalar(ws_place[:, :, :], ws_place[:, :, :], ws_col[:, :], -1.0, ALU.mult, ALU.mult).then_inc(ws_ready, 1)
            dve.tensor_scalar(bs_neg[:, :], bs_neg[:, :], -1.0, None, ALU.mult).then_inc(ws_ready, 1)
            dve.wait_ge(ws_ready, 2)
            dve.wait_ge(scoresT_psum, 1)
            dve.tensor_copy(tok_rowsT[:, :], bank_out[0:2 * B, 0:128]).then_inc(scoresT_ready, 1)

            dve.wait_ge(rows_loaded, 16 * 4)
            with dve.Fori(0, B) as b:
                for t in range(2):
                    k = 2 * b + t
                    row = score_rows[:, bass.ds(b * N, N)]
                    me = tok_score[:, bass.ds(k, 1)]
                    dve.tensor_scalar(cmp_junk[:, 0:N], row, me, None, ALU.is_gt, ALU.add,
                                      accum_out=above[:, bass.ds(k, 1)]).then_inc(compared, 1)
                    dve.wait_ge(compared, 4 * b + 2 * t + 1)
                    dve.scalar_tensor_tensor(cmp_junk[:, 0:N], row, me, earlier[:, t, :], ALU.is_equal, ALU.mult,
                                             accum_out=ties[:, bass.ds(k, 1)]).then_inc(compared, 1)
                    dve.wait_ge(compared, 4 * b + 2 * t + 2)
            dve.tensor_tensor(rank[:, :], above[:, :], ties[:, :], ALU.add).then_inc(rank_ready, 1)
            dve.wait_ge(rank_ready, 1)
            with dve.Fori(0, B // 2) as i:
                for par in range(2):
                    b = 2 * i + par
                    dve.wait_ge(picked, b + 1)
                    for t in range(2):
                        ins = dve.tensor_scalar(onehot[:, par, t, :], iota_keep[:, :], rank[:, bass.ds(2 * b + t, 1)],
                                                None, ALU.is_equal)
                    ins.then_inc(onehot_ready, 1)

            def tile_stats(slot):
                for t, rows in TILES:
                    ins = dve.bn_stats(stats[0:rows, 2 * slot + t, :], resid[0:rows, slot, t, :])
                return ins

            with dve.Fori(0, B) as b:
                dve.wait_ge(resid_ready, b + 3)
                tile_stats(b + 1).then_inc(stats_done, 1)

            steps = [0]

            def link(ins):
                steps[0] += 1
                ins.then_inc(ln_step, 1)
                dve.wait_ge(ln_step, steps[0])

            def finish_stats(n):
                mE, mO, vE, vO = (stats[:, :, c] for c in (1, 4, 2, 5))
                dve.tensor_tensor(mean[:, :], mE, mO, ALU.add)
                dve.tensor_tensor(diff[:, :], mE, mO, ALU.subtract)
                link(dve.tensor_tensor(var[:, :], vE, vO, ALU.add))
                dve.tensor_scalar(mean[:, :], mean[:, :], 0.5, None, ALU.mult)
                dve.tensor_scalar(var[:, :], var[:, :], 1.0 / D, EPS, ALU.mult, ALU.add)
                link(dve.scalar_tensor_tensor(diff[:, :], diff[:, :], 0.25, diff[:, :], ALU.mult, ALU.mult))
                dve.tensor_tensor(var[:, :], var[:, :], diff[:, :], ALU.add).then_inc(var_ready, 1)
                dve.wait_ge(std_ready, n)
                link(dve.reciprocal(rstd[:, :], std[:, :]))
                link(dve.tensor_tensor(newt[:, :], rstd[:, :], rstd[:, :], ALU.mult))
                link(dve.tensor_tensor(newt[:, :], newt[:, :], var[:, :], ALU.mult))
                link(dve.tensor_scalar(newt[:, :], newt[:, :], -0.5, 1.5, ALU.mult, ALU.add))
                link(dve.tensor_tensor(rstd[:, :], rstd[:, :], newt[:, :], ALU.mult))

            dve.wait_ge(stats_done, B)
            finish_stats(1)

            def normalise(slot):
                for t, rows in TILES:
                    k = 2 * slot + t
                    ins = dve.tensor_scalar(normed[0:rows, t, :], resid[0:rows, slot, t, :],
                                            mean[0:rows, bass.ds(k, 1)], rstd[0:rows, bass.ds(k, 1)],
                                            ALU.subtract, ALU.mult)
                return ins

            def pre_norm(c):
                normalise(c + 1).then_inc(normed_ready, 1)

            def pre_xT(c):
                dve.wait_ge(xT_psum, c + 1)
                dve.tensor_copy(xT[0][:, :], bank_pre[:, 0:KEEP])
                dve.tensor_copy(xT[1][0:DB, :], bank_pre[0:DB, KEEP:2 * KEEP]).then_inc(xT_ready, 1)

            def pre_qk(c, par):
                dve.wait_ge(q_psum, c + 1)
                q = q_cols[par]
                dve.tensor_copy(q[:, 0:UA], bank_pre[:, 0:KEEP])
                dve.tensor_copy(q[0:64, UA:UNITS], bank_pre[0:64, KEEP:2 * KEEP:2])
                dve.tensor_copy(q[64:128, UA:UNITS - 1], bank_pre[64:128, KEEP + 1:2 * KEEP:2]).then_inc(q_ready, 1)
                dve.wait_ge(k_psum, c + 1)
                dve.tensor_copy(k_sb[par][:, :], bank_k[par][:, 0:2 * KEEP]).then_inc(k_ready, 1)

            def pre_v(c, par):
                dve.wait_ge(v_psum, c + 1)
                for t, rows in TILES:
                    ins = dve.tensor_copy(v_sb[par][0:rows, t, :, 0:HD],
                                          bank_pre[0:rows, t * D:(t + 1) * D].rearrange("p (h d) -> p h d", d=HD))
                ins.then_inc(v_ready, 1)

            def turn_out(b, par, c):
                last = min(CHUNK * c + CHUNK, GROUPS) - 1
                cols = (last + 1 - CHUNK * c) * 128
                dve.wait_ge(turned, b * GROUPS + last + 5)
                dve.tensor_copy(pt[par][0][:, CHUNK * c * 128:CHUNK * c * 128 + cols], bank_pt[0][:, 0:cols])
                dve.tensor_copy(pt[par][1][0:TB, CHUNK * c * 128:CHUNK * c * 128 + cols],
                                bank_pt[1][0:TB, 0:cols]).then_inc(pt_ready, 1)

            def ctx_out(b):
                dve.wait_ge(ctx_psum, b + 1)
                for t, rows in TILES:
                    c = bank_out[0:rows, t * HEADS * VC:(t + 1) * HEADS * VC].rearrange("p (h v) -> p h v", v=VC)
                    ins = dve.reciprocal(inv_sum[0:rows, t, :], c[:, :, HD])
                ins.then_inc(ctx_inv, 1)
                dve.wait_ge(ctx_inv, b + 1)
                for t, rows in TILES:
                    c = bank_out[0:rows, t * HEADS * VC:(t + 1) * HEADS * VC].rearrange("p (h v) -> p h v", v=VC)
                    ins = dve.tensor_tensor(ctx_sb[0:rows, t, :].rearrange("p (h d) -> p h d", d=HD), c[:, :, 0:HD],
                                            inv_sum[0:rows, t, :].unsqueeze(2).to_broadcast([rows, HEADS, HD]), ALU.mult)
                ins.then_inc(ctx_ready, 1)

            def ctxT_out(b):
                dve.wait_ge(ctxT_psum, b + 1)
                dve.tensor_copy(ctxT[0][:, :], bank_out[:, 0:KEEP])
                dve.tensor_copy(ctxT[1][0:DB, :], bank_out[0:DB, KEEP:2 * KEEP]).then_inc(ctxT_ready, 1)

            def add_out(b):
                dve.wait_ge(proj_psum, b + 1)
                for t, rows in TILES:
                    ins = dve.tensor_tensor(resid[0:rows, b, t, :], resid[0:rows, b, t, :],
                                            bank_out[0:rows, t * D:(t + 1) * D], ALU.add)
                ins.then_inc(resid_added, 1)
                dve.wait_ge(resid_added, 2 * b + 1)
                tile_stats(b).then_inc(resid_added, 1)

            def dve_sums(b, par, g):
                n = b * GROUPS + g
                if g == 0:
                    dve.wait_ge(q_ready, b + 1)
                dve.wait_ge(tanh_done, n + 1)
                sums(dve, args[(par * GROUPS + g) % 2], bank_k[par], q_cols[par], g, 0, DVE_UNITS).then_inc(args_dve, 1)

            def smax(b, par, g):
                n = b * GROUPS + g
                slot = (par * GROUPS + g) % 2
                dve.wait_ge(scored, n + 1)
                dve.wait_ge(exp_done, n + 1)
                dve.tensor_scalar(s_sb[slot][:, :], bank_s[slot][:, 0:KEEP], bs_neg[:, :], None, ALU.add, ALU.min,
                                  accum_out=s_min[slot][:, :]).then_inc(smax_done, 1)

            def lagging(b, par, g, last=False):
                if g == 3:
                    turn_out(b - 1, 1 - par, 3)
                if g == 4:
                    turn_out(b - 1, 1 - par, 4)
                if g == 11:
                    ctx_out(b)
                if g == 13:
                    ctxT_out(b)
                if g == 15:
                    add_out(b)
                if last:
                    return
                if g in (8, 12, 16):
                    turn_out(b, par, g // 4 - 2)
                if g == 9:
                    pre_norm(b + 1)
                if g == 12:
                    pre_xT(b + 1)
                if g == 14:
                    pre_qk(b + 1, 1 - par)
                if g == 16:
                    pre_v(b + 1, 1 - par)

            dve.wait_ge(wf_loaded, 16 * 7)
            wlink = [0]

            def wchain(ins):
                wlink[0] += 1
                ins.then_inc(w_step, 1)
                dve.wait_ge(w_step, wlink[0])

            wchain(dve.memset(w_max[:, :], 0.0))
            dve.tensor_reduce(w_max[:, 0:1], w1q[0][:, :], AX.X, ALU.max, apply_absolute_value=True)
            wchain(dve.tensor_reduce(w_max[:, 2:3], w2f[:, :, :], AX.XY, ALU.max, apply_absolute_value=True))
            wchain(dve.tensor_reduce(w_max[0:DB, 1:2], w1q[1][:, :], AX.X, ALU.max, apply_absolute_value=True))
            dve.tensor_tensor(w_maxes[:, 0:1], w_max[:, 0:1], w_max[:, 1:2], ALU.max)
            dve.tensor_copy(w_maxes[:, 1:2], w_max[:, 2:3]).then_inc(w_maxed, 1)
            dve.reciprocal(inv_gelu[:, :], s_gelu[:, :])
            wchain(dve.reciprocal(inv_out[:, :], s_out[:, :]))
            dve.wait_ge(w_alled, 1)
            wchain(dve.tensor_scalar(w_scale[:, :], w_all[:, :], 1.0 / 127.0, None, ALU.mult))
            wchain(dve.reciprocal(w_inv[:, :], w_scale[:, :]))
            wchain(dve.tensor_tensor(y_scale[:, :], s_gelu[:, :], w_scale[:, 1:2], ALU.mult))
            dve.tensor_tensor(y_scale[:, :], y_scale[:, :], inv_out[:, :], ALU.mult)
            dve.tensor_scalar(b2_row[:, :], b2_row[:, :], inv_out[:, :], None, ALU.mult)
            for rows, w, m, o in ((DA, w1q[0][:, :], 0, w1q[0][:, :]), (DB, w1q[1][:, :], 0, w1q[1][:, :]),
                                  (128, w2f[:, :, :], 1, w2q[:, :, :])):
                wchain(dve.tensor_scalar(w, w, w_inv[0:rows, m:m + 1], -127.0, ALU.mult, ALU.max))
                wchain(dve.tensor_scalar(w, w, 127.0, MAGIC, ALU.min, ALU.add))
                wchain(dve.tensor_scalar(o, w, MAGIC, None, ALU.subtract))

            dve.memset(pt[1][0], 1.0)
            dve.memset(pt[1][1][0:TB, :], 1.0)
            pre_norm(0)
            pre_xT(0)
            pre_qk(0, 0)
            pre_v(0, 0)
            with dve.Fori(0, B // 2) as i:
                for par in range(2):
                    b = 2 * i + par
                    for g in range(GROUPS):
                        dve_sums(b, par, g)
                        smax(b, par, g)
                        lagging(b, par, g)
            for g in range(GROUPS):
                if g < 2:
                    smax(B, 0, g)
                lagging(B, 0, g, last=True)

            dve.wait_ge(resid_added, 2 * (B + 1))
            finish_stats(2)

            def ffn_norm(i, par):
                for t, rows in TILES:
                    k = 2 * (i + 1) + t
                    ins = dve.tensor_scalar(fnorm[par][0:rows, t, :], resid[0:rows, i + 1, t, :],
                                            mean[0:rows, bass.ds(k, 1)], rstd[0:rows, bass.ds(k, 1)],
                                            ALU.subtract, ALU.mult)
                ins.then_inc(f_normed, 1)

            def ffn_step(i, par):
                if real(i + 2):
                    dve.wait_ge(f_xT_psum, i + 1)
                    ffn_norm(i + 2, par)
                if real(i - 2):
                    b = i - 2
                    dve.wait_ge(y_psum, b + 1)
                    n = 3 * b
                    for t, rows in TILES:
                        ins = dve.scalar_tensor_tensor(y_sb[0:rows, t, :], bank_out[0:rows, t * D:(t + 1) * D],
                                                       y_scale[0:rows, :], b2_row[0:rows, :], ALU.mult, ALU.add)
                    ins.then_inc(y_step, 1)
                    dve.wait_ge(y_step, n + 1)
                    for t, rows in TILES:
                        ins = dve.tensor_scalar(y_sb[0:rows, t, :], y_sb[0:rows, t, :], -128.0, 127.0, ALU.max, ALU.min)
                    ins.then_inc(y_step, 1)
                    dve.wait_ge(y_step, n + 2)
                    for t, rows in TILES:
                        ins = dve.tensor_scalar(y_sb[0:rows, t, :], y_sb[0:rows, t, :], MAGIC, MAGIC, ALU.add, ALU.subtract)
                    ins.then_inc(y_step, 1)
                    dve.wait_ge(y_step, n + 3)
                    for t, rows in TILES:
                        r = resid[0:rows, b + 1, t, :]
                        ins = dve.scalar_tensor_tensor(r, y_sb[0:rows, t, :], s_out[0:rows, :], r, ALU.mult, ALU.add)
                    ins.then_inc(f_added, 1)
                    dve.wait_ge(f_added, 2 * b + 1)
                    tile_stats(b + 1).then_inc(f_added, 1)
                if real(i - 1):
                    b = i - 1
                    g, q = gelu[1 - par], hq[1 - par]
                    dve.wait_ge(gelu_done, b + 1)
                    dve.tensor_scalar(g, g, inv_gelu[:, :], -128.0, ALU.mult, ALU.max).then_inc(quant_step, 1)
                    dve.wait_ge(quant_step, 2 * b + 1)
                    dve.tensor_scalar(g, g, 127.0, MAGIC, ALU.min, ALU.add).then_inc(quant_step, 1)
                    dve.wait_ge(quant_step, 2 * b + 2)
                    if not isinstance(b, int) or b >= 2:
                        dve.wait_ge(y_psum, b - 1)
                    dve.tensor_scalar(q, g, MAGIC, None, ALU.subtract).then_inc(hq_ready, 1)

            ffn_norm(0, 0)
            ffn_norm(1, 1)
            staged(dve, ffn_step, (2, 2))

            dve.wait_ge(f_added, 2 * B)
            finish_stats(3)
            dve.wait_ge(w1_step, 3)
            dve.wait_ge(qv_blank, 4)
            with dve.Fori(0, B) as b:
                for t, rows in TILES:
                    k = 2 * (b + 1) + t
                    ins = dve.tensor_scalar(xn3[0:rows, bass.ds(k - 2, 1), :].rearrange("p o d -> p (o d)"),
                                            resid[0:rows, b + 1, t, :],
                                            mean[0:rows, bass.ds(k, 1)], rstd[0:rows, bass.ds(k, 1)],
                                            ALU.subtract, ALU.mult)
                ins.then_inc(n3_step, 1)
                dve.wait_ge(n3_step, 2 * b + 1)
                for t, rows in TILES:
                    ins = dve.tensor_reduce(mx3[0:rows, bass.ds(2 * b + t, 1)],
                                            xn3[0:rows, bass.ds(2 * b + t, 1), :].rearrange("p o d -> p (o d)"),
                                            AX.X, ALU.max, apply_absolute_value=True)
                ins.then_inc(n3_step, 1)
            dve.wait_ge(n3_step, 2 * B)
            dve.tensor_reduce(x_max[:, :], mx3[:, :], AX.X, ALU.max).then_inc(x_maxed, 1)
            dve.wait_ge(x_alled, 1)
            dve.tensor_scalar(x_scale[:, :], x_allmax[:, :], 1.0 / 127.0, 1e-8, ALU.mult, ALU.max).then_inc(x3_step, 1)
            dve.wait_ge(x3_step, 1)
            dve.reciprocal(x_inv[:, :], x_scale[:, :]).then_inc(x3_step, 1)
            dve.wait_ge(x3_step, 2)
            for t, rows in TILES:
                part = xn3[0:rows, t::2, :]
                ins = dve.tensor_scalar(part, part, x_inv[0:rows, :], -128.0, ALU.mult, ALU.max)
            ins.then_inc(x3_step, 1)
            dve.wait_ge(x3_step, 3)
            for t, rows in TILES:
                part = xn3[0:rows, t::2, :]
                ins = dve.tensor_scalar(part, part, 127.0, MAGIC, ALU.min, ALU.add)
            ins.then_inc(x3_step, 1)
            dve.wait_ge(x3_step, 4)

            def xq_make(c, par):
                need(dve, xqT_psum, c - 1)
                for t, rows in TILES:
                    ins = dve.tensor_scalar(xq[par][0:rows, t, :],
                                            xn3[0:rows, bass.ds(2 * c + t, 1), :].rearrange("p o d -> p (o d)"),
                                            MAGIC, None, ALU.subtract)
                ins.then_inc(xq_ready, 1)

            def q_out(c, par, fill):
                dve.wait_ge(qkv_psum, 4 * c + fill + 1)
                for col in range(2):
                    src = bank_pre[:, col * KEEP:(col + 1) * KEEP]
                    kind, r = (0, col) if fill == 0 else (col, 2)
                    dst = (q1 if kind == 0 else k1)[par][:, r, 0:KEEP]
                    ins = dve.tensor_scalar(dst, src, x_scale[:, :], bqk1[kind][:, r:r + 1], ALU.mult, ALU.add)
                ins.then_inc(qkv_out, 1)

            def v_out(c, par):
                dve.wait_ge(qkv_psum, 4 * c + 4)
                for t, rows in TILES:
                    ins = dve.scalar_tensor_tensor(
                        v1[par][0:rows, t, :, 0:HD],
                        bank_pre[0:rows, t * D:(t + 1) * D].rearrange("p (h d) -> p h d", d=HD), x_scale[0:rows, :],
                        bv1[0:rows, :].rearrange("p (h d) -> p h d", d=HD), ALU.mult, ALU.add)
                ins.then_inc(qkv_out, 1)

            def ctx1_divide(b, lo, hi, k):
                n = hi - lo
                dve.wait_ge(ctx1_tokens, 2 * b + k + 1)
                for t, rows in TILES:
                    c = bank_out[0:rows, t * 128 * n:(t + 1) * 128 * n].rearrange("p (h v) -> p h v", v=32)
                    ins = dve.reciprocal(inv_sum[0:rows, t, 4 * lo:4 * hi], c[:, :, HD])
                ins.then_inc(ctx1_inv, 1)
                dve.wait_ge(ctx1_inv, 2 * b + k + 1)
                for t, rows in TILES:
                    c = bank_out[0:rows, t * 128 * n:(t + 1) * 128 * n].rearrange("p (h v) -> p h v", v=32)
                    ins = dve.tensor_tensor(
                        ctx_sb[0:rows, t, 4 * lo * HD:4 * hi * HD].rearrange("p (h d) -> p h d", d=HD), c[:, :, 0:HD],
                        inv_sum[0:rows, t, 4 * lo:4 * hi].unsqueeze(2).to_broadcast([rows, 4 * n, HD]), ALU.mult)
                ins.then_inc(ctx1_ready, 1)

            def attn1_step(b, par):
                for u in range(PAIRS):
                    n, slot = PAIRS * b + u, u % 2
                    if u == 0 and real(b - 2):
                        dve.wait_ge(proj1_psum, b - 1)
                        for t, rows in TILES:
                            r = resid[0:rows, b - 1, t, :]
                            ins = dve.tensor_tensor(r, r, bank_out[0:rows, t * D:(t + 1) * D], ALU.add)
                        ins.then_inc(added1, 1)
                    if real(n, PAIRS * B):
                        dve.wait_ge(pair_scored, n + 1)
                        need(dve, pair_scaled, n - 1)
                        dve.tensor_reduce(pmax[slot][:, :, :], pair_banks[slot], AX.X, ALU.max).then_inc(pair_maxed, 1)
                        dve.wait_ge(pair_maxed, n + 1)
                        dve.tensor_scalar(pneg[slot][:, :], pmax[slot][:, :, :].rearrange("p e t -> p (e t)"),
                                          -C2 * 2.0 ** 23, None, ALU.mult).then_inc(pair_neg, 1)
                    if real(n - 1, PAIRS * B):
                        other = p1[1 - slot].bitcast(I32)
                        dve.wait_ge(pair_scaled, n)
                        need(dve, pair_turned, n - 2)
                        dve.tensor_scalar(other, y1[1 - slot], -1.0, -126.0 * 2.0 ** 23, ALU.min, ALU.max).then_inc(pair_clipped, 1)
                        dve.wait_ge(pair_clipped, n)
                        dve.tensor_scalar(other, other, -(1 << 30), None, ALU.bitwise_xor).then_inc(pair_powered, 1)
                    if u == 1 and real(b - 1):
                        ctx1_divide(b - 1, 0, 2, 0)
                    if u == 3 and real(b - 1):
                        ctx1_divide(b - 1, 2, 3, 1)
                    if u == 1 and real(b - 2):
                        dve.wait_ge(added1, 2 * b - 3)
                        tile_stats(b - 1).then_inc(added1, 1)
                    if not real(b + 1):
                        continue
                    if u == 0:
                        xq_make(b + 1, 1 - par)
                    if u in (2, 4):
                        q_out(b + 1, 1 - par, u - 2)
                    if u == 5:
                        v_out(b + 1, 1 - par)

            xq_make(0, 0)
            q_out(0, 0, 0)
            q_out(0, 0, 2)
            v_out(0, 0)
            staged(dve, attn1_step, (1, 2))

            dve.wait_ge(added1, 2 * B)
            finish_stats(4)
            dve.wait_ge(e_consts, 4)
            logits, hot, work_a, work_b = gate
            dve.memset(logits, 0.0).then_inc(g_step, 1)
            dve.wait_ge(g_step, 1)

            def gate_step(i, par):
                if real(i):
                    for t, rows in TILES:
                        k = 2 * (i + 1) + t
                        ins = dve.tensor_scalar(xn4[0:rows, bass.ds(k - 2, 1), :].rearrange("p o d -> p (o d)"),
                                                resid[0:rows, i + 1, t, :],
                                                mean[0:rows, bass.ds(k, 1)], rstd[0:rows, bass.ds(k, 1)],
                                                ALU.subtract, ALU.mult)
                    ins.then_inc(n4_ready, 1)
                    dve.wait_ge(n4_ready, 2 * i + 1)
                    need(dve, gxT_psum, i - 1)
                    for t, rows in TILES:
                        ins = dve.tensor_copy(fnorm[par][0:rows, t, :],
                                              xn4[0:rows, bass.ds(2 * i + t, 1), :].rearrange("p o d -> p (o d)"))
                    ins.then_inc(n4_ready, 1)
                if real(i - 2):
                    dve.wait_ge(gate_psum, i - 1)
                    for t, rows in TILES:
                        ins = dve.tensor_copy(logits[0:rows, :, bass.ds(2 * (i - 2) + t, 1)].rearrange("p e o -> p (e o)"),
                                              bank_s[par][0:rows, t * EXPERTS:(t + 1) * EXPERTS])
                    ins.then_inc(gate_out, 1)

            staged(dve, gate_step, (0, 2))

            gsteps = [1]

            def glink(ins):
                gsteps[0] += 1
                ins.then_inc(g_step, 1)
                dve.wait_ge(g_step, gsteps[0])

            ek = [128, EXPERTS, 2 * B]
            by_token = "p e k -> p k e"
            over_k = lambda a: a[:, :].unsqueeze(2).to_broadcast(ek)
            over_e = lambda a: a[:, :].unsqueeze(1).to_broadcast(ek)
            dve.wait_ge(gate_out, B)
            glink(dve.tensor_reduce(top[:, :], logits.rearrange(by_token), AX.X, ALU.max))
            glink(dve.tensor_tensor(hot, logits, over_e(top), ALU.is_ge))
            glink(dve.tensor_tensor(hot, hot, over_k(iota_e), ALU.mult))
            glink(dve.tensor_reduce(top[:, :], hot.rearrange(by_token), AX.X, ALU.min))
            glink(dve.tensor_tensor(hot, over_k(iota_e), over_e(top), ALU.is_equal))
            dve.tensor_tensor(hot, hot, over_e(valid), ALU.mult).then_inc(chosen, 1)
            dve.wait_ge(prefix_psum, 1)
            flat = "p e k -> p (e k)"
            glink(dve.tensor_copy(work_a.rearrange(flat), bank_pt[1][:, 0:KE]))
            glink(dve.tensor_tensor_scan(work_b.rearrange(flat), carry[:, :, :].rearrange(flat), work_a.rearrange(flat),
                                         0.0, ALU.mult, ALU.add))
            dve.tensor_tensor(work_a, work_b, work_a, ALU.subtract)
            glink(dve.tensor_copy(counts_i[:, :], work_b[:, :, 2 * B - 1]))
            glink(dve.tensor_scalar(counts_i[:, :], counts_i[:, :], 127.0, None, ALU.add))
            glink(dve.tensor_scalar(counts_i[:, :], counts_i[:, :], 7, None, ALU.arith_shift_right))
            glink(dve.tensor_copy(tiles_f[:, :], counts_i[:, :]))
            glink(dve.tensor_tensor_scan(ends[:, :], ones[:, 0:EXPERTS], tiles_f[:, :], 0.0, ALU.mult, ALU.add))
            glink(dve.tensor_tensor(base[:, :], ends[:, :], tiles_f[:, :], ALU.subtract))
            xe = [128, XT, EXPERTS]
            glink(dve.tensor_tensor(ended[:, :, :], iota_t[:, :].unsqueeze(2).to_broadcast(xe),
                                    ends[:, :].unsqueeze(1).to_broadcast(xe), ALU.is_ge))
            glink(dve.tensor_reduce(owner[:, :], ended[:, :, :], AX.X, ALU.add))
            dve.tensor_scalar(owner_i[:, :], owner[:, :], float(EXPERTS - 1), None, ALU.min)
            glink(dve.tensor_scalar(base[:, :], base[:, :], 128.0, None, ALU.mult))
            glink(dve.tensor_tensor(work_b.rearrange(flat), work_a.rearrange(flat), bank_pt[0][:, 0:KE], ALU.add))
            glink(dve.tensor_tensor(work_b, work_b, over_k(base), ALU.add))
            glink(dve.tensor_tensor(work_b, work_b, hot, ALU.mult))
            glink(dve.tensor_reduce(slot_f[:, :], work_b.rearrange(by_token), AX.X, ALU.add))
            dve.tensor_copy(slot_i[:, :], slot_f[:, :]).then_inc(slots_ready, 1)

            def expert_step(i, par):
                if real(i, XT):
                    dve.wait_ge(exT_psum, i + 1)
                    need(dve, eh_psum, i - 1)
                    dve.tensor_copy(exT[par][0][:, :], bank_k[par][:, 0:128])
                    dve.tensor_copy(exT[par][1][0:DB, :], bank_k[par][0:DB, 128:256]).then_inc(exT_ready, 1)
                if real(i - 2, XT):
                    dve.wait_ge(ehT_psum, i - 1)
                    need(dve, ey_psum, i - 3)
                    dve.tensor_copy(ehT[par][0][:, :], bank_pt[par][:, 0:128])
                    dve.tensor_copy(ehT[par][1][0:DB, :], bank_pt[par][0:DB, 128:256]).then_inc(ehT_ready, 1)

            staged(dve, expert_step, (0, 4), XT)
            for b in range(B):
                dve.wait_ge(back[b % 4], 32 * (b // 4 + 1))
                for t, rows in TILES:
                    r = resid[0:rows, b + 1, t, :]
                    ins = dve.tensor_tensor(r, r, xn4[0:rows, 2 * b + t, :], ALU.add)
                ins.then_inc(summed, 1)

        @block.tensor
        def _(pe):
            pe.wait_ge(scores_ready, 1)
            pe.wait_ge(consts, 1)
            pe.transpose(bank_out[0:2 * B, 0:128], tok_score[:, :], ident[:, :]).then_inc(scoresT_psum, 1)
            pe.sem_inc(picked, 2)
            with pe.Fori(0, B // 2) as i:
                for par in range(2):
                    b = 2 * i + par
                    pe.wait_ge(onehot_ready, b + 1)
                    pe.wait_ge(resid_ready, b + 1)
                    for t, rows in TILES:
                        for h in range(2):
                            ins = pe.matmul(bank_k[par][0:rows, t * D:(t + 1) * D],
                                            onehot[:, par, h, t * TA:t * TA + rows],
                                            x_all[:, bass.ds(2 * b + h, 1), :].rearrange("p o d -> p (o d)"),
                                            start=(h == 0), stop=(h == 1))
                    ins.then_inc(picked, 1)

            pe.wait_ge(w0_loaded, 16 * 18)
            pe.wait_ge(ws_ready, 2)
            pe.sem_inc(scored, 2)
            pe.sem_inc(turned, 1)

            def turn_tokens(bank, src):
                for r, (lo, hi) in enumerate(((0, DA), (DA, D))):
                    for t, rows in TILES:
                        ins = pe.transpose(bank[0:hi - lo, r * KEEP + t * TA:r * KEEP + t * TA + rows],
                                           src[0:rows, t, lo:hi], ident[0:rows, 0:rows])
                return ins

            def product(out, lhs, rhs):
                pe.matmul(out, lhs[0], rhs[0], start=True, stop=False)
                return pe.matmul(out, lhs[1], rhs[1], start=False, stop=True)

            def pre_turn(c):
                pe.wait_ge(normed_ready, c + 1)
                if not isinstance(c, int):
                    pe.wait_ge(v_ready, c)
                turn_tokens(bank_pre, normed).then_inc(xT_psum, 1)

            def pre_qk_mm(c, par):
                pe.wait_ge(xT_ready, c + 1)
                x = (xT[0][:, :], xT[1][:, :])
                for h in range(2):
                    ins = product(bank_pre[:, h * KEEP:(h + 1) * KEEP], [w[:, 128 * h:128 * h + 128] for w in wq0], x)
                ins.then_inc(q_psum, 1)
                for h in range(2):
                    ins = product(bank_k[par][:, h * KEEP:(h + 1) * KEEP], [w[:, 128 * h:128 * h + 128] for w in wk0], x)
                ins.then_inc(k_psum, 1)

            def pre_v_mm(c):
                pe.wait_ge(q_ready, c + 1)
                for t, rows in TILES:
                    ins = product(bank_pre[0:rows, t * D:(t + 1) * D],
                                  [x[:, t * TA:t * TA + rows] for x in xT], [w[:, :] for w in wv0])
                ins.then_inc(v_psum, 1)

            def score_group(b, par, g):
                n = b * GROUPS + g
                slot = (par * GROUPS + g) % 2
                pe.wait_ge(tanh_done, n + 3)
                pe.wait_ge(smax_done, n + 1)
                for j in range(4):
                    for quad in range(4):
                        u = 4 * quad + j
                        if u < units(g):
                            ins = pe.matmul(bank_s[slot][32 * quad:32 * quad + 32, 0:KEEP], ws_place[:, j, :],
                                            tanhs[slot][:, u * KEEP:(u + 1) * KEEP],
                                            start=(j == 0), stop=(j == 3 or u + 1 >= units(g)))
                ins.then_inc(scored, 1)

            def turn_group(b, par, g):
                n = b * GROUPS + g
                pslot = (par * GROUPS + g - 3) % 2
                bb, gg = (b, g - 3) if g >= 3 else (b - 1, g - 3 + GROUPS)
                c, k = gg // CHUNK, gg % CHUNK
                pe.wait_ge(exp_done, n + 2)
                if k == 0:
                    pe.wait_ge(pt_ready, CHUNKS * bb + c + 2)
                pe.transpose(bank_pt[0][:, 128 * k:128 * k + 128], p_sb[pslot][:, 0:TA], ident[:, :])
                pe.transpose(bank_pt[1][0:TB, 128 * k:128 * k + 128], p_sb[pslot][:, TA:KEEP],
                             ident[:, :]).then_inc(turned, 1)

            def head_cols(h, t0, rows):
                first, step = (h, 8) if h < 8 else (8 * UA + h - 8, 4)
                return slice(first + step * t0, first + step * (t0 + rows - 1) + 1, step)

            def context(b, par, heads):
                for h in heads:
                    for t, rows in TILES:
                        o = bank_out[0:rows, t * HEADS * VC + h * VC:t * HEADS * VC + (h + 1) * VC]
                        for s, srows in TILES:
                            ins = pe.matmul(o, pt[1 - par][s][0:srows, head_cols(h, t * TA, rows)],
                                            v_sb[1 - par][0:srows, s, h, :], start=(s == 0), stop=(s == 1))
                return ins

            def lagging(b, par, g, last=False):
                if not last or g < 3:
                    turn_group(b, par, g)
                if g == 4:
                    pe.wait_ge(pt_ready, CHUNKS * b + 2)
                if 4 <= g < 10:
                    ins = context(b, par, (2 * g - 8, 2 * g - 7))
                if g == 9:
                    ins.then_inc(ctx_psum, 1)
                if g == 11:
                    pe.wait_ge(ctx_ready, b + 1)
                    turn_tokens(bank_out, ctx_sb).then_inc(ctxT_psum, 1)
                if g == 13:
                    pe.wait_ge(ctxT_ready, b + 1)
                    for t, rows in TILES:
                        ins = product(bank_out[0:rows, t * D:(t + 1) * D],
                                      [x[:, t * TA:t * TA + rows] for x in ctxT], [w[:, :] for w in wo0])
                    ins.then_inc(proj_psum, 1)
                if last:
                    return
                if g == 10:
                    pre_turn(b + 1)
                if g == 12:
                    pre_qk_mm(b + 1, 1 - par)
                if g == 14:
                    pre_v_mm(b + 1)

            pre_turn(0)
            pre_qk_mm(0, 0)
            pre_v_mm(0)
            with pe.Fori(0, B // 2) as i:
                for par in range(2):
                    b = 2 * i + par
                    for g in range(GROUPS):
                        score_group(b, par, g)
                        lagging(b, par, g)
            for g in range(GROUPS):
                lagging(B, 0, g, last=True)

            def ffn_step(i, par):
                if real(i + 1):
                    pe.wait_ge(f_normed, i + 2)
                    if not isinstance(i, int) or i >= 0:
                        pe.wait_ge(f_xT_ready, i + 1)
                    turn_tokens(bank_pre, fnorm[1 - par]).then_inc(f_xT_psum, 1)
                if real(i):
                    pe.wait_ge(f_xT_ready, i + 1)
                    if not isinstance(i, int) or i >= 2:
                        pe.wait_ge(gelu_done, i - 1)
                    for c in range(HT):
                        o = ffn_banks[par][c // 2][:, c % 2 * KEEP:(c % 2 + 1) * KEEP]
                        ins = product(o, [w[:, c * 128:(c + 1) * 128] for w in w1q], [x[:, :] for x in fx[par]])
                        if c % 2:
                            ins.then_inc(h_psum, 1)
                if real(i - 1):
                    b = i - 1
                    pe.wait_ge(hq_ready, b + 1)
                    if not isinstance(b, int) or b >= 1:
                        pe.wait_ge(f_added, 2 * b - 1)
                    for t, rows in TILES:
                        for c in range(HT):
                            ins = pe.matmul(bank_out[0:rows, t * D:(t + 1) * D],
                                            hq[1 - par][:, c * KEEP + t * TA:c * KEEP + t * TA + rows], w2q[:, c, :],
                                            start=(c == 0), stop=(c == HT - 1))
                    ins.then_inc(y_psum, 1)

            ffn_step(-1, 1)
            staged(pe, ffn_step, (1, 1))

            def xq_turn(c, par):
                pe.wait_ge(xq_ready, c + 1)
                need(pe, qkv_out, 4 * c)
                b16 = bank_pre.bitcast(BF16)
                for r, (lo, hi) in enumerate(((0, DA), (DA, D))):
                    for t, rows in TILES:
                        ins = pe.transpose(b16[0:hi - lo, r * 256 + t * TA:r * 256 + t * TA + rows],
                                           xq[par][0:rows, t, lo:hi], ident16[0:rows, 0:rows])
                ins.then_inc(xqT_psum, 1)

            def split_product(pairs):
                out, terms = pairs
                for n, (lhs, rhs) in enumerate(terms):
                    ins = pe.matmul(out, lhs, rhs, start=(n == 0), stop=(n == len(terms) - 1))
                return ins

            def qkv_mm(c, par, fill):
                if fill == 0:
                    pe.wait_ge(xqT_ready, c + 1)
                else:
                    pe.wait_ge(qkv_out, 4 * c + fill)
                x = xqT[par]
                if fill < 3:
                    for col in range(2):
                        kind, r = ((0, col), (1, col), (col, 2))[fill]
                        ins = split_product((bank_pre[:, col * KEEP:(col + 1) * KEEP],
                                             [(w1parts[kind][m][h][:, 128 * r:128 * r + 128], x[h][:, :])
                                              for m in range(3) for h in range(2)]))
                else:
                    for t, rows in TILES:
                        ins = split_product((bank_pre[0:rows, t * D:(t + 1) * D],
                                             [(x[h][:, t * TA:t * TA + rows], w1parts[2][m][h][:, :])
                                              for m in range(3) for h in range(2)]))
                ins.then_inc(qkv_psum, 1)

            def context1(b, par, r, col):
                for s, srows in TILES:
                    for j in range(4):
                        h = 4 * r + j
                        ins = pe.matmul(bank_out[32 * j:32 * j + 32, col * KEEP:(col + 1) * KEEP],
                                        v1[par][0:srows, s, h, :], pt1[par][s][0:srows, h * KEEP:(h + 1) * KEEP],
                                        start=(s == 0), stop=(s == 1))
                return ins

            def context1_turn(b, lo, hi, k):
                pe.wait_ge(ctx1_out, 2 * b + k + 1)
                n = hi - lo
                for t, rows in TILES:
                    for r in range(lo, hi):
                        c = t * 128 * n + (r - lo) * 128
                        ins = pe.transpose(bank_out[0:rows, c:c + 128],
                                           ctx1[:, r * KEEP + t * TA:r * KEEP + t * TA + rows], ident[:, :])
                ins.then_inc(ctx1_tokens, 1)

            def attn1_step(b, par):
                for u in range(PAIRS):
                    n, slot = PAIRS * b + u, u % 2
                    if real(n, PAIRS * B):
                        if u == 0:
                            pe.wait_ge(qkv_out, 4 * b + 3)
                        need(pe, pair_scaled, n - 1)
                        for t in range(2):
                            for e in range(2):
                                r, j = (2 * u + e) // 4, (2 * u + e) % 4
                                ins = pe.matmul(pair_banks[slot][:, e, t, :],
                                                q1[par][32 * j:32 * j + 32, r, t * TA:(t + 1) * TA],
                                                k1[par][32 * j:32 * j + 32, r, :], start=True, stop=True)
                        ins.then_inc(pair_scored, 1)
                    m = n - 2
                    if real(m, PAIRS * B):
                        pe.wait_ge(pair_powered, m + 1)
                        need(pe, pair_pt, m)
                        p = p1[slot].rearrange("p (e t s) -> p e t s", e=2, t=2)
                        for e in range(2):
                            for s, srows in TILES:
                                for t, rows in TILES:
                                    c = e * KEEP + t * TA
                                    ins = pe.transpose(bank_pt[s][0:srows, c:c + rows],
                                                       p[0:rows, e, t, s * TA:s * TA + srows], ident[0:rows, 0:rows])
                        ins.then_inc(pair_turned, 1)
                    if real(b - 1):
                        if u == 0:
                            need(pe, added1, 2 * b - 3)
                            pe.wait_ge(pair_pt, PAIRS * (b - 1) + 4)
                            pe.wait_ge(qkv_out, 4 * b)
                            context1(b - 1, 1 - par, 0, 0)
                            context1(b - 1, 1 - par, 1, 1).then_inc(ctx1_psum, 1)
                        if u == 1:
                            context1_turn(b - 1, 0, 2, 0)
                        if u == 2:
                            pe.wait_ge(pair_pt, PAIRS * b)
                            pe.wait_ge(ctx1_ready, 2 * b - 1)
                            context1(b - 1, 1 - par, 2, 0).then_inc(ctx1_psum, 1)
                        if u == 3:
                            context1_turn(b - 1, 2, 3, 1)
                        if u == 4:
                            pe.wait_ge(ctx1_ready, 2 * b)
                            turn_tokens(bank_out, ctx_sb).then_inc(ctx1T_psum, 1)
                        if u == 5:
                            pe.wait_ge(ctx1T_ready, b)
                            for t, rows in TILES:
                                ins = product(bank_out[0:rows, t * D:(t + 1) * D],
                                              [x[:, t * TA:t * TA + rows] for x in ctxT], [w[:, :] for w in wo1])
                            ins.then_inc(proj1_psum, 1)
                    if real(b + 1):
                        if u == 1:
                            xq_turn(b + 1, 1 - par)
                        if u >= 2:
                            qkv_mm(b + 1, 1 - par, u - 2)

            pe.wait_ge(w1_ready, 1)
            pe.wait_ge(w1_loaded, 16 * 18)
            xq_turn(0, 0)
            for fill in range(4):
                qkv_mm(0, 0, fill)
            staged(pe, attn1_step, (1, 1))

            pe.wait_ge(e_loaded, 16 * 9)

            def gate_step(i, par):
                if real(i):
                    pe.wait_ge(n4_ready, 2 * i + 2)
                    need(pe, gxT_ready, i - 1)
                    turn_tokens(bank_k[par], fnorm[par]).then_inc(gxT_psum, 1)
                if real(i - 1):
                    pe.wait_ge(gxT_ready, i)
                    need(pe, gate_out, i - 2)
                    for t, rows in TILES:
                        ins = product(bank_s[1 - par][0:rows, t * EXPERTS:(t + 1) * EXPERTS],
                                      [x[:, t * TA:t * TA + rows] for x in gxT[1 - par]], [w[:, :] for w in wg])
                    ins.then_inc(gate_psum, 1)

            staged(pe, gate_step, (0, 1))
            pe.wait_ge(chosen, 1)
            hot = gate[1].rearrange("p e k -> p (e k)")
            pe.matmul(bank_pt[0][:, 0:KE], lower[:, :], hot, start=True, stop=True)
            pe.matmul(bank_pt[1][:, 0:KE], ones[:, :], hot, start=True, stop=True).then_inc(prefix_psum, 1)

            def turn_tile(bank, src):
                pe.transpose(bank[:, 0:128], src[:, 0:DA], ident[:, :])
                return pe.transpose(bank[0:DB, 128:256], src[:, DA:D], ident[:, :])

            def expert_product(o, lhs, w, tile):
                e = pe.value_load(owner_i[0:1, bass.ds(tile, 1)], min_val=0, max_val=EXPERTS - 1)
                pe.matmul(o, lhs[0][:, :], w[0][:, bass.ds(e * D, D)], start=True, stop=False)
                return pe.matmul(o, lhs[1][:, :], w[1][:, bass.ds(e * D, D)], start=False, stop=True)

            pe.wait_ge(slots_ready, 1)

            def expert_step(i, par):
                if real(i, XT):
                    pe.wait_ge(xs_loaded[par], 8 * (i - par) + 16)
                    need(pe, exT_ready, i - 1)
                    turn_tile(bank_k[par], xs[par]).then_inc(exT_psum, 1)
                if real(i - 1, XT):
                    pe.wait_ge(exT_ready, i)
                    need(pe, eh_ready, i - 2)
                    expert_product(bank_s[1 - par][:, 0:D], exT[1 - par], ew1, i - 1).then_inc(eh_psum, 1)
                if real(i - 2, XT):
                    pe.wait_ge(eh_ready, i - 1)
                    need(pe, ehT_ready, i - 3)
                    turn_tile(bank_pt[par], eh[par]).then_inc(ehT_psum, 1)
                if real(i - 3, XT):
                    pe.wait_ge(ehT_ready, i - 2)
                    need(pe, ey_ready, i - 4)
                    expert_product(out_banks[1 - par][:, 0:D], ehT[1 - par], ew2, i - 3).then_inc(ey_psum, 1)

            staged(pe, expert_step, (0, 5), XT)


_TURNED = ["L0_attn_Wq", "L0_attn_Wk", "L0_attn_Wv", "L0_attn_Wo", "L0_ffn_W1", "L0_ffn_W2",
           "L1_ffn_W1", "L1_ffn_W2", "L1_ffn_Wg"]
_COLS = {"L0_ffn_b1": 128, "L1_attn_bq": 4 * HD, "L1_attn_bk": 4 * HD}
_INS = ["x", "L0_tok_w", "L0_tok_b", "L0_attn_bq", "L0_attn_bk", "L0_attn_bv", "L0_attn_bo", "L0_attn_ws", "L0_attn_bs",
        "L0_ffn_b2", "L0_ffn_s_gelu", "L0_ffn_s_out",
        "L1_attn_Wq", "L1_attn_Wk", "L1_attn_Wv", "L1_attn_Wo", "L1_attn_bv", "L1_attn_bo",
        "L1_ffn_b1", "L1_ffn_b2", "L1_ffn_bg"]


def kernel(**inputs):
    import numpy as _np
    import concourse.bacc as _bacc
    from concourse import mybir as _mybir
    from concourse.bass_utils import run_bass_kernel_spmd as _run

    nc = _bacc.Bacc("TRN2", target_bir_lowering=False, num_devices=1)
    arrays, aps = {}, {}
    for name in _INS + _TURNED + list(_COLS):
        a = _np.asarray(inputs[name])
        if name in _COLS:
            a = a.reshape(-1, _COLS[name]).T
            name += "_cols"
        if name in _TURNED:
            a = _np.swapaxes(a, -1, -2)
            name += "T"
        a = _np.ascontiguousarray(a)
        arrays[f"in_{name}"] = a
        aps[name] = nc.dram_tensor(f"in_{name}", a.shape, _mybir.dt.from_np(a.dtype), kind="ExternalInput").ap()
    out = nc.dram_tensor("out", (B, KEEP, D), F32, kind="ExternalOutput").ap()
    build(nc, aps, out)
    r = _run(nc, [arrays], core_ids=[0])
    return r.results[0]["out"]
```

```python
from contextlib import ExitStack

import concourse.bass as bass
from concourse import mybir

F32 = mybir.dt.float32
BF16 = mybir.dt.bfloat16
I32 = mybir.dt.int32
U32 = mybir.dt.uint32
U8 = mybir.dt.uint8
ALU = mybir.AluOpType
ACT = mybir.ActivationFunctionType
AX = mybir.AxisListType
RMAX = bass.bass_isa.ReduceOp.max

B, N, D = 16, 256, 192
KEEP = int(round(N * 0.7))
TA = 128
TB = KEEP - TA
TILES = ((0, TA), (1, TB))
HEADS, HD = 12, 16
DA, DB = 128, D - 128
SLOTS = B + 2
ROWS = 2 * SLOTS

UA = KEEP
UB = (KEEP + 1) // 2
UNITS = UA + UB
UG = 16
GROUPS = -(-UNITS // UG)
BODY = 2 * GROUPS
DVE_UNITS = 9
CHUNK = 4
CHUNKS = -(-GROUPS // CHUNK)
PT_COLS = GROUPS * 128
VC = HD + 1
EPS = 1e-5
HID = 4 * D
HT = HID // 128
HW = HT * KEEP
C2 = 1.4426950408889634
ROUNDS = HEADS // 4
PAIRS = HEADS // 2
EXPERTS = 16
XT = (B * KEEP + EXPERTS * 127) // 128
MAGIC = 1.5 * 2.0 ** 23


def build(nc, I, out):
    ctx = ExitStack()
    with ctx:
        def sb(name, shape, dt=F32):
            return ctx.enter_context(nc.sbuf_tensor(name, shape, dt))

        def ps(name):
            return ctx.enter_context(nc.psum_tensor(name, [128, 512], F32))

        def sem(name):
            return ctx.enter_context(nc.semaphore(name))

        resid = sb("resid", [128, SLOTS, 2, D])
        work = sb("work", [128, 12288])
        x_all = work[:, 0:2 * B * D].rearrange("p (k d) -> p k d", d=D)
        x_prod = work[:, 2 * B * D:4 * B * D].rearrange("p (k d) -> p k d", d=D)
        cmp_junk = [work[:, 2 * B * D + 64 * n:2 * B * D + 64 * (n + 1)].bitcast(U8) for n in range(16)]
        arg_slots = [work[:, n * UG * KEEP:(n + 1) * UG * KEEP] for n in range(4)]

        def arg_slot(k):
            return arg_slots[k % 4], (BODY % 4 or 4) if k < BODY % 4 else 4

        pt_region = sb("pt_region", [128, 9216])
        pt = [[pt_region[:, (2 * n + m) * PT_COLS:(2 * n + m + 1) * PT_COLS] for m in range(2)] for n in range(2)]
        score_rows = pt_region[:, 0:B * N]

        shared = sb("shared", [128, 4352])
        carved = [0]

        def carve(shape):
            size = 1
            for n in shape[1:]:
                size *= n
            a = shared[0:shape[0], carved[0]:carved[0] + size]
            carved[0] += size
            if len(shape) == 2:
                return a
            names = "abc"[:len(shape) - 1]
            dims = {c: n for c, n in zip(names[1:], shape[2:])}
            return a.rearrange(f"p ({' '.join(names)}) -> p {' '.join(names)}", **dims)

        ident = sb("ident", [128, 128])
        iota_keep = sb("iota_keep", [128, KEEP])
        earlier = carve([128, 2, N])
        tok_w = sb("tok_w", [128, D])
        tok_b = sb("tok_b", [128, 1])
        ws_col = sb("ws_col", [128, 1])
        bs_neg = sb("bs_neg", [128, 1])
        ws_place = sb("ws_place", [128, 4, 32])
        wq0 = [carve([DA, 256]), carve([DB + 1, 256])]
        wk0 = [carve([DA, 256]), carve([DB + 1, 256])]
        wv0 = [sb("wv0a", [DA, D]), sb("wv0b", [DB + 1, D])]
        wo0 = [sb("wo0a", [DA, D]), sb("wo0b", [DB + 1, D])]

        tok_score = sb("tok_score", [128, 2 * B])
        tok_rowsT = sb("tok_rowsT", [2 * B, 128])
        above = sb("above", [128, 2 * B])
        ties = sb("ties", [128, 2 * B])
        rank = sb("rank", [128, 2 * B])
        onehot = carve([128, 2, 2, KEEP])
        stats = sb("stats", [128, ROWS, 6])
        mean = sb("mean", [128, ROWS])
        diff = sb("diff", [128, ROWS])
        var = sb("var", [128, ROWS])
        std = sb("std", [128, ROWS])
        rstd = sb("rstd", [128, ROWS])
        newt = sb("newt", [128, ROWS])
        normed = sb("normed", [128, 2, D])
        xT = [sb("xTa", [DA, KEEP]), sb("xTb", [DB + 1, KEEP])]
        q_cols = [carve([128, UNITS + 1]) for n in range(2)]
        k_sb = [carve([128, 2 * KEEP]) for n in range(2)]
        v_sb = [carve([128, 2, HEADS, VC]) for n in range(2)]
        s_sb = [sb(f"s_sb{n}", [128, KEEP]) for n in range(2)]
        s_min = [sb(f"s_min{n}", [128, 1]) for n in range(2)]
        p_sb = [sb(f"p_sb{n}", [128, KEEP]) for n in range(2)]
        inv_sum = sb("inv_sum", [128, 2, HEADS])
        ctx_sb = sb("ctx_sb", [128, 2, D])
        ctxT = [sb("ctxTa", [DA, KEEP]), sb("ctxTb", [DB + 1, KEEP])]

        w1q = [sb("w1qa", [DA, HID]), sb("w1qb", [DB, HID])]
        w2f = sb("w2f", [128, HT, D])
        w2q = sb("w2q", [128, HT, D], BF16)
        b1_col = sb("b1_col", [128, HT])
        b2_row = sb("b2_row", [128, D])
        s_gelu = sb("s_gelu", [128, 1])
        s_out = sb("s_out", [128, 1])
        w_max = sb("w_max", [128, 3])
        w_maxes = sb("w_maxes", [128, 2])
        w_all = sb("w_all", [128, 2])
        w_scale = sb("w_scale", [128, 2])
        w_inv = sb("w_inv", [128, 2])
        inv_gelu = sb("inv_gelu", [128, 1])
        inv_out = sb("inv_out", [128, 1])
        y_scale = sb("y_scale", [128, 1])
        fx = [[sb(f"fx{n}a", [DA, KEEP]), sb(f"fx{n}b", [DB, KEEP])] for n in range(2)]
        fnorm = [normed, sb("fnorm1", [128, 2, D])]
        gelu = [pt_region[:, n * HW:(n + 1) * HW] for n in range(2)]
        hq = [pt_region[:, 2 * HW + n * HW // 2:2 * HW + (n + 1) * HW // 2].bitcast(BF16) for n in range(2)]
        y_sb = sb("y_sb", [128, 2, D])

        psum = ctx.enter_context(nc.psum_tensor("psum", [128, 8 * 512], F32))
        bank_k0, bank_k1, bank_s0, bank_s1, bank_pta, bank_ptb, bank_pre, bank_out = (
            psum[:, 512 * n:512 * n + 512] for n in range(8))
        bank_k, bank_s, bank_pt = [bank_k0, bank_k1], [bank_s0, bank_s1], [bank_pta, bank_ptb]
        pair_banks = [psum[:, 1024 * n:1024 * n + 1024].rearrange("p (e c) -> p e c", e=2)[:, :, 0:2 * KEEP]
                      .rearrange("p e (t s) -> p e t s", t=2) for n in range(2)]

        xn3 = work[:, 0:2 * B * D].rearrange("p (k d) -> p k d", d=D)
        y1 = [work[:, 2 * B * D + n * 4 * KEEP:2 * B * D + (n + 1) * 4 * KEEP] for n in range(2)]
        p1 = [work[:, 2 * B * D + (n + 2) * 4 * KEEP:2 * B * D + (n + 3) * 4 * KEEP] for n in range(2)]
        ctx1 = work[:, 2 * B * D + 16 * KEEP:2 * B * D + 19 * KEEP]
        PT1 = HEADS * KEEP
        pt1 = [[pt_region[:, (2 * n + m) * PT1:(2 * n + m + 1) * PT1] for m in range(2)] for n in range(2)]
        ew1 = [pt_region[:, 0:EXPERTS * D], pt_region[0:DB + 1, EXPERTS * D:2 * EXPERTS * D]]
        ew2 = [work[:, 2 * EXPERTS * D:3 * EXPERTS * D], work[0:DB + 1, 3 * EXPERTS * D:4 * EXPERTS * D]]
        xn4 = xn3
        KE = 2 * B * EXPERTS
        wg = [sb("wga", [DA, EXPERTS]), sb("wgb", [DB + 1, EXPERTS])]
        carved[0] = 0
        lower = carve([128, 128])
        ones = carve([128, 128])
        valid = sb("valid", [128, 2 * B])
        iota_e = sb("iota_e", [128, EXPERTS])
        iota_t = sb("iota_t", [128, XT])
        carry = carve([128, EXPERTS, 2 * B])
        gate = [pt_region[:, c:c + KE].rearrange("p (e k) -> p e k", e=EXPERTS)
                for c in (4 * PT_COLS, 2 * B * D, 2 * B * D + KE, 2 * B * D + 2 * KE)]
        xs = [pt_region[:, 2 * B * D + 3 * KE + n * D:2 * B * D + 3 * KE + (n + 1) * D] for n in range(4)]
        tile_w = [[[pt_region[0:rows, 2 * B * D + (4 * m + 2 * n + r) * D:2 * B * D + (4 * m + 2 * n + r + 1) * D]
                    for r, rows in enumerate((DA, DB + 1))] for n in range(2)] for m in range(2)]
        tstats = sb("tstats", [128, 4, 6])
        tmean = sb("tmean", [128, 4])
        trstd = sb("trstd", [128, 4])
        tnum = sb("tnum", [128, 7, 4])
        tsum, tdiff, tvar, thalf, tbits = (sb(f"t{n}", [128, 4]) for n in ("sum", "diff", "var", "half", "bits"))
        top = sb("top", [128, 2 * B])
        counts = sb("counts", [128, EXPERTS])
        counts_i = sb("counts_i", [128, EXPERTS], I32)
        tiles_f = sb("tiles_f", [128, EXPERTS])
        ends = sb("ends", [128, EXPERTS])
        base = sb("base", [128, EXPERTS])
        ended = carve([128, XT, EXPERTS])
        owner = sb("owner", [128, XT])
        owner_i = sb("owner_i", [128, XT], I32)
        slot_f = sb("slot_f", [128, 2 * B])
        slot_i = sb("slot_i", [128, 2 * B], U32)
        zeros = sb("zeros", [128, D])
        exT = [[carve([DA, 128]), carve([DB + 1, 128])] for n in range(2)]
        eh = [carve([128, D]) for n in range(2)]
        ehT = [[carve([DA, 128]), carve([DB + 1, 128])] for n in range(2)]
        ey = [carve([128, D]) for n in range(4)]
        xs_dram = nc.dram_tensor("xs_dram", (XT * 128, D), F32, kind="Internal").ap()
        ys_dram = nc.dram_tensor("ys_dram", (XT * 128, D), F32, kind="Internal").ap()
        ident16 = sb("ident16", [128, 128], BF16)
        wsrc = [[sb(f"wsrc{n}a", [DA, D]), sb(f"wsrc{n}b", [DB, D])] for n in range(3)]
        wrest = sb("wrest", [128, D])
        w1parts = [[[sb(f"w1p{n}{m}{r}", [rows, HEADS * (32 if n < 2 else HD)], BF16) for r, rows in enumerate((DA, DB))]
                    for m in range(3)] for n in range(3)]
        wo1 = [sb("wo1a", [DA, D]), sb("wo1b", [DB + 1, D])]
        bqk1 = [sb(f"bqk1{n}", [128, ROUNDS]) for n in range(2)]
        bv1 = sb("bv1", [128, D])
        mx3 = sb("mx3", [128, 2 * B])
        x_max = sb("x_max", [128, 1])
        x_allmax = sb("x_allmax", [128, 1])
        x_scale = sb("x_scale", [128, 1])
        x_inv = sb("x_inv", [128, 1])
        xq = [sb(f"xq{n}", [128, 2, D], BF16) for n in range(2)]
        xqT = [[sb(f"xqT{n}a", [DA, KEEP], BF16), sb(f"xqT{n}b", [DB, KEEP], BF16)] for n in range(2)]
        carved[0] = 0
        q1 = [carve([128, ROUNDS, 2 * TA]) for n in range(2)]
        k1 = [carve([128, ROUNDS, KEEP]) for n in range(2)]
        v1 = [carve([128, 2, HEADS, 32]) for n in range(2)]
        pmax = [sb(f"pmax{n}", [128, 2, 2]) for n in range(2)]
        pneg = [sb(f"pneg{n}", [128, 4]) for n in range(2)]

        out_banks = [bank_pre, bank_out]
        ffn_banks = [[bank_k[0], bank_k[1], bank_s[0]], [bank_s[1], bank_pt[0], bank_pt[1]]]

        scores_dram = nc.dram_tensor("scores_dram", (2 * B, 128), F32, kind="Internal").ap()

        x_loaded = sem("x_loaded")
        small_loaded = sem("small_loaded")
        w0_loaded = sem("w0_loaded")
        consts = sem("consts")
        const_step = sem("const_step")
        ws_ready = sem("ws_ready")
        dots_done = sem("dots_done")
        scores_ready = sem("scores_ready")
        scoresT_psum = sem("scoresT_psum")
        scoresT_ready = sem("scoresT_ready")
        scores_stored = sem("scores_stored")
        rows_loaded = sem("rows_loaded")
        compared = sem("compared")
        rank_ready = sem("rank_ready")
        onehot_ready = sem("onehot_ready")
        picked = sem("picked")
        resid_ready = sem("resid_ready")
        filled = sem("filled")
        stats_done = sem("stats_done")
        ln_step = sem("ln_step")
        var_ready = sem("var_ready")
        std_ready = sem("std_ready")
        ln_ready = sem("ln_ready")

        normed_ready = sem("normed_ready")
        xT_psum = sem("xT_psum")
        xT_ready = sem("xT_ready")
        q_psum = sem("q_psum")
        k_psum = sem("k_psum")
        q_ready = sem("q_ready")
        k_ready = sem("k_ready")
        v_psum = sem("v_psum")
        v_ready = sem("v_ready")
        args_dve = sem("args_dve")
        args_pool = sem("args_pool")
        tanh_done = sem("tanh_done")
        scored = sem("scored")
        smax_done = sem("smax_done")
        exp_done = sem("exp_done")
        turned = sem("turned")
        pt_ready = sem("pt_ready")
        ctx_psum = sem("ctx_psum")
        ctx_inv = sem("ctx_inv")
        ctx_ready = sem("ctx_ready")
        ctxT_psum = sem("ctxT_psum")
        ctxT_ready = sem("ctxT_ready")
        proj_psum = sem("proj_psum")
        resid_added = sem("resid_added")
        stored = sem("stored")

        wf_loaded = sem("wf_loaded")
        w_step = sem("w_step")
        w_maxed = sem("w_maxed")
        w_alled = sem("w_alled")
        w_scaled = sem("w_scaled")
        wq_step = sem("wq_step")
        f_normed = sem("f_normed")
        f_xT_psum = sem("f_xT_psum")
        f_xT_ready = sem("f_xT_ready")
        h_psum = sem("h_psum")
        gelu_done = sem("gelu_done")
        quant_step = sem("quant_step")
        hq_ready = sem("hq_ready")
        y_psum = sem("y_psum")
        y_step = sem("y_step")
        f_added = sem("f_added")
        w1_loaded = sem("w1_loaded")
        w1_step = sem("w1_step")
        w1_ready = sem("w1_ready")
        qv_blank = sem("qv_blank")
        n3_step = sem("n3_step")
        x_maxed = sem("x_maxed")
        x_alled = sem("x_alled")
        x3_step = sem("x3_step")
        xq_ready = sem("xq_ready")
        xqT_psum = sem("xqT_psum")
        xqT_ready = sem("xqT_ready")
        qkv_psum = sem("qkv_psum")
        qkv_out = sem("qkv_out")
        pair_scored = sem("pair_scored")
        pair_maxed = sem("pair_maxed")
        pair_neg = sem("pair_neg")
        pair_scaled = sem("pair_scaled")
        pair_clipped = sem("pair_clipped")
        pair_powered = sem("pair_powered")
        pair_turned = sem("pair_turned")
        pair_pt = sem("pair_pt")
        ctx1_psum = sem("ctx1_psum")
        ctx1_out = sem("ctx1_out")
        ctx1_tokens = sem("ctx1_tokens")
        ctx1_inv = sem("ctx1_inv")
        ctx1_ready = sem("ctx1_ready")
        ctx1T_psum = sem("ctx1T_psum")
        ctx1T_ready = sem("ctx1T_ready")
        proj1_psum = sem("proj1_psum")
        added1 = sem("added1")
        e_consts = sem("e_consts")
        e_zeroed = sem("e_zeroed")
        e_loaded = sem("e_loaded")
        n4_ready = sem("n4_ready")
        gxT_psum = sem("gxT_psum")
        gxT_ready = sem("gxT_ready")
        gate_psum = sem("gate_psum")
        gate_out = sem("gate_out")
        g_step = sem("g_step")
        chosen = sem("chosen")
        prefix_psum = sem("prefix_psum")
        slots_ready = sem("slots_ready")
        sent = sem("sent")
        xs_loaded = [sem(f"xs_loaded{n}") for n in range(4)]
        exT_psum = sem("exT_psum")
        w1_fetched = sem("w1_fetched")
        exT_ready = sem("exT_ready")
        eh_psum = sem("eh_psum")
        eh_ready = sem("eh_ready")
        ehT_psum = sem("ehT_psum")
        ehT_ready = sem("ehT_ready")
        ey_psum = sem("ey_psum")
        ey_ready = sem("ey_ready")
        ys_stored = [sem(f"ys_stored{n}") for n in range(4)]
        pair_stats = sem("pair_stats")
        pair_step = sem("pair_step")
        stats_taken = sem("stats_taken")
        pair_norm = sem("pair_norm")
        norm_used = sem("norm_used")
        tnum_ready = sem("tnum_ready")
        xq_step = sem("xq_step")
        back = [sem(f"back{n}") for n in range(4)]
        summed = sem("summed")

        block = ctx.enter_context(nc.Block())

        def units(g):
            return min(UG, UNITS - g * UG)

        def parts(g, lo, hi):
            hi = min(hi, units(g))
            cut = min(max(UA - g * UG, lo), hi)
            return [(h, a, e) for h, a, e in ((0, lo, cut), (1, cut, hi)) if e > a]

        def sums(eng, dst, k, q, g, lo, hi):
            for h, a, e in parts(g, lo, hi):
                ins = eng.tensor_tensor(
                    dst[:, a * KEEP:e * KEEP].rearrange("p (u s) -> p u s", s=KEEP),
                    k[:, h * KEEP:(h + 1) * KEEP].unsqueeze(1).to_broadcast([128, e - a, KEEP]),
                    q[:, g * UG + a:g * UG + e].unsqueeze(2).to_broadcast([128, e - a, KEEP]), ALU.add)
            return ins

        def staged(eng, step, lags, count=B, body=2):
            ahead, behind = lags
            first = -(-max(4, behind) // body) * body
            last = (count - ahead) // body * body
            for i in range(first):
                step(i, i % body)
            with eng.Fori(first // body, last // body) as j:
                for par in range(body):
                    step(body * j + par, par)
            for i in range(last, count + behind):
                step(i, i % body)

        def real(b, count=B):
            return not isinstance(b, int) or 0 <= b < count

        def need(eng, sem, value):
            if not isinstance(value, int) or value > 0:
                eng.wait_ge(sem, value)

        @block.sync
        def _(sp):
            xv = I["x"].rearrange("b (t p) d -> p (b t) d", p=128)
            for n in range(4):
                sp.dma_start(x_all[:, 8 * n:8 * n + 8, :], xv[:, 8 * n:8 * n + 8, :]).then_inc(x_loaded, 16)
            for r, (lo, hi) in enumerate(((0, DA), (DA, D))):
                sp.dma_start(w1q[r][:, :], I["L0_ffn_W1T"][lo:hi, :]).then_inc(wf_loaded, 16)
            sp.dma_start(w2f[:, :, :], I["L0_ffn_W2T"].rearrange("(c p) d -> p c d", p=128)).then_inc(wf_loaded, 16)
            sp.dma_start(b1_col[:, :], I["L0_ffn_b1_cols"]).then_inc(wf_loaded, 16)
            sp.dma_start(b2_row[:, :], I["L0_ffn_b2"].partition_broadcast(128)).then_inc(wf_loaded, 16)
            sp.dma_start(s_gelu[:, :], I["L0_ffn_s_gelu"].partition_broadcast(128)).then_inc(wf_loaded, 16)
            sp.dma_start(s_out[:, :], I["L0_ffn_s_out"].partition_broadcast(128)).then_inc(wf_loaded, 16)
            sp.wait_ge(scoresT_ready, 1)
            sp.dma_start(scores_dram, tok_rowsT[:, :]).then_inc(scores_stored, 16)
            sp.wait_ge(scores_stored, 16)
            flat = scores_dram.rearrange("k p -> (k p)")
            for n in range(4):
                cols = slice(n * B * N // 4, (n + 1) * B * N // 4)
                sp.dma_start(score_rows[:, cols], flat[cols].partition_broadcast(128)).then_inc(rows_loaded, 16)
            for n, name in enumerate("qkv"):
                for r, (lo, hi) in enumerate(((0, DA), (DA, D))):
                    sp.dma_start(wsrc[n][r][:, :], I[f"L1_attn_W{name}"][lo:hi, :]).then_inc(w1_loaded, 16)
            sp.dma_start(bv1[:, :], I["L1_attn_bv"].partition_broadcast(128)).then_inc(w1_loaded, 16)
            for r, (lo, hi) in enumerate(((0, DA), (DA, D))):
                sp.dma_start(wo1[r][0:hi - lo, :], I["L1_attn_Wo"][lo:hi, :]).then_inc(w1_loaded, 16)
            sp.dma_start(wo1[1][DB:DB + 1, :], I["L1_attn_bo"].rearrange("(o d) -> o d", o=1)).then_inc(w1_loaded, 16)
            sp.wait_ge(w1_step, 2)
            for j in range(4):
                for n, name in enumerate("qk"):
                    sp.dma_start(bqk1[n][32 * j:32 * j + HD, :],
                                 I[f"L1_attn_b{name}_cols"][HD * j:HD * j + HD, :]).then_inc(w1_loaded, 16)
            sp.wait_ge(e_consts, 1)
            sp.dma_start(xs_dram.rearrange("(j p) d -> p j d", p=128),
                         zeros[:, :].unsqueeze(1).to_broadcast([128, XT, D])).then_inc(e_zeroed, 16)
            for r, (lo, hi) in enumerate(((0, DA), (DA, D))):
                sp.dma_start(wg[r][0:hi - lo, :], I["L1_ffn_WgT"][lo:hi, :]).then_inc(e_loaded, 16)
            sp.dma_start(wg[1][DB:DB + 1, :], I["L1_ffn_bg"].rearrange("(o d) -> o d", o=1)).then_inc(e_loaded, 16)
            sp.wait_ge(added1, B)
            for dst, wt, bias in ((ew1, "L1_ffn_W1T", "L1_ffn_b1"), (ew2, "L1_ffn_W2T", "L1_ffn_b2")):
                for r, (lo, hi) in enumerate(((0, DA), (DA, D))):
                    sp.dma_start(dst[r][0:hi - lo, :].rearrange("p (e h) -> p e h", h=D),
                                 I[wt][:, lo:hi, :].rearrange("e p h -> p e h")).then_inc(e_loaded, 16)
                sp.dma_start(dst[1][DB:DB + 1, :], I[bias].rearrange("(o e) d -> o (e d)", o=1)).then_inc(e_loaded, 16)

            sp.wait_ge(sent, 16 * 2 * B)

            def expert_step(i, par):
                if real(i, XT):
                    need(sp, exT_psum, i - 3)
                    sp.dma_start(xs[par][:, :], xs_dram[bass.ds(128 * i, 128), :]).then_inc(xs_loaded[par], 16)

            staged(sp, expert_step, (0, 0), XT, 4)
            for b in range(B):
                sp.wait_ge(summed, b + 1)
                for t, rows in TILES:
                    sp.dma_start(out[b, t * TA:t * TA + rows, :], resid[0:rows, b + 1, t, :]).then_inc(stored, 16)
            sp.wait_ge(stored, 16 * 2 * B)

        @block.gpsimd
        def _(pool):
            step = [0]

            def chain(ins):
                step[0] += 1
                ins.then_inc(const_step, 1)
                pool.wait_ge(const_step, step[0])

            chain(pool.memset(ident[:, :], 0.0))
            chain(pool.affine_select(out=ident[:, :], in_=ident[:, :], compare_op=ALU.not_equal, fill=1.0,
                                     base=0, pattern=[[-1, 128]], channel_multiplier=1))
            pool.iota(iota_keep[:, :], pattern=[[1, KEEP]], base=0, channel_multiplier=0,
                      allow_small_or_imprecise_dtypes=True)
            chain(pool.memset(earlier[:, :, :], 1.0))
            chain(pool.affine_select(out=earlier[:, :, :], in_=earlier[:, :, :], compare_op=ALU.is_gt, fill=0.0,
                                     base=0, pattern=[[128, 2], [-1, N]], channel_multiplier=1))
            chain(pool.memset(ws_place[:, :, :], 1.0))
            chain(pool.affine_select(out=ws_place[:, :, :], in_=ws_place[:, :, :], compare_op=ALU.is_ge, fill=0.0,
                                     base=0, pattern=[[8 * HD, 4], [-HD, 32]], channel_multiplier=1))
            pool.affine_select(out=ws_place[:, :, :], in_=ws_place[:, :, :], compare_op=ALU.is_ge, fill=0.0,
                               base=HD - 1, pattern=[[-8 * HD, 4], [HD, 32]],
                               channel_multiplier=-1).then_inc(consts, 1)

            for n in range(2):
                pool.memset(bqk1[n][:, :], 0.0).then_inc(w1_step, 1)
            pool.tensor_copy(ident16[:, :], ident[:, :])
            for n in range(2):
                for m in range(3):
                    for r in range(2):
                        pool.memset(w1parts[n][m][r][:, :], 0.0)
            pool.memset(mx3[:, :], 0.0).then_inc(w1_step, 1)

            pool.memset(zeros[:, :], 0.0).then_inc(e_consts, 1)
            for n, value in enumerate((0.5, 1.0 / D, 0.25, EPS, -0.5, 1597463007.0, 1.5)):
                ins = pool.memset(tnum[:, n, :], value)
            ins.then_inc(tnum_ready, 1)
            pool.wait_ge(w_maxed, 1)
            pool.partition_all_reduce(w_all[:, :], w_maxes[:, :], 128, RMAX).then_inc(w_alled, 1)
            pool.wait_ge(w_scaled, 1)
            quant = [0]

            def qchain(ins):
                quant[0] += 1
                ins.then_inc(wq_step, 1)
                pool.wait_ge(wq_step, quant[0])

            for rows, w, m, o in ((DA, w1q[0][:, :], 0, w1q[0][:, :]), (DB, w1q[1][:, :], 0, w1q[1][:, :]),
                                  (128, w2f[:, :, :], 1, w2q[:, :, :])):
                qchain(pool.tensor_scalar(w, w, w_inv[0:rows, m:m + 1], -127.0, ALU.mult, ALU.max))
                qchain(pool.tensor_scalar(w, w, 127.0, MAGIC, ALU.min, ALU.add))
                qchain(pool.tensor_scalar(o, w, MAGIC, None, ALU.subtract))

            def pool_sums(b, par, g):
                n = b * GROUPS + g
                if g == 0:
                    pool.wait_ge(q_ready, b + 1)
                    pool.wait_ge(k_ready, b + 1)
                slot, back_to = arg_slot(par * GROUPS + g)
                pool.wait_ge(scored, n + 3 - back_to)
                sums(pool, slot, k_sb[par], q_cols[par], g, DVE_UNITS, UG).then_inc(args_pool, 1)

            pool.wait_ge(picked, B + 2)
            with pool.Fori(0, B // 2) as i:
                for par in range(2):
                    for g in range(GROUPS):
                        pool_sums(2 * i + par, par, g)

            pool.wait_ge(w1_loaded, 16 * 18)
            pool.wait_ge(w1_step, 3)
            at = [3]

            def chain1(ins):
                at[0] += 1
                ins.then_inc(w1_step, 1)
                pool.wait_ge(w1_step, at[0])

            for n in range(3):
                for r, rows in enumerate((DA, DB)):
                    src = wsrc[n][r][:, :].rearrange("p (h d) -> p h d", d=HD)
                    rest = wrest[0:rows, :].rearrange("p (h d) -> p h d", d=HD)
                    for m in range(3):
                        part = w1parts[n][m][r][:, :].rearrange("p (h c) -> p h c", h=HEADS)[:, :, 0:HD]
                        chain1(pool.tensor_copy(part, src))
                        if m < 2:
                            chain1(pool.tensor_tensor(rest, src, part, ALU.subtract))
                            src = rest
            pool.sem_inc(w1_ready, 1)
            pool.wait_ge(args_pool, B * GROUPS)
            pool.wait_ge(resid_added, 2 * (B + 1))
            for n in range(2):
                pool.memset(q1[n][:, :, :], 0.0)
                pool.memset(v1[n][:, :, :, :], 0.0).then_inc(qv_blank, 1)
            pool.wait_ge(qv_blank, 2)
            for n in range(2):
                pool.memset(v1[n][:, :, :, HD:HD + 1], 1.0).then_inc(qv_blank, 1)

            half, over_d, quarter, eps, minus_half, guess, one_half = (tnum[:, n, :] for n in range(7))
            pool.wait_ge(tnum_ready, 1)
            LINKS = 20

            def pair_norms(j, phase):
                at = [0]

                def link(ins):
                    at[0] += 1
                    ins.then_inc(pair_step, 1)
                    pool.wait_ge(pair_step, (j + phase * B // 2) * LINKS + at[0])

                mE, mO, vE, vO = (tstats[:, :, c] for c in (1, 4, 2, 5))
                s, d, v, h, g, y = (a[:, :] for a in (tsum, tdiff, tvar, thalf, tbits, trstd))
                pool.wait_ge(pair_stats, 2 * j + phase * B + 2)
                pool.tensor_tensor(s, mE, mO, ALU.add)
                pool.tensor_tensor(d, mE, mO, ALU.subtract)
                link(pool.tensor_tensor(v, vE, vO, ALU.add))
                pool.sem_inc(stats_taken, 2)
                pool.tensor_tensor(v, v, over_d, ALU.mult)
                link(pool.tensor_tensor(d, d, d, ALU.mult))
                pool.tensor_tensor(d, d, quarter, ALU.mult)
                link(pool.tensor_tensor(v, v, eps, ALU.add))
                link(pool.tensor_tensor(v, v, d, ALU.add))
                pool.wait_ge(norm_used, 2 * j + phase * B + 2)
                pool.tensor_tensor(tmean[:, :], s, half, ALU.mult)
                link(pool.tensor_copy(g, v.bitcast(I32)))
                link(pool.tensor_tensor(g, g, minus_half, ALU.mult))
                link(pool.tensor_tensor(g, g, guess, ALU.add))
                pool.tensor_tensor(h, v, minus_half, ALU.mult)
                link(pool.tensor_copy(y.bitcast(I32), g))
                for n in range(3):
                    link(pool.tensor_tensor(s, y, y, ALU.mult))
                    link(pool.tensor_tensor(s, s, h, ALU.mult))
                    link(pool.tensor_tensor(s, s, one_half, ALU.add))
                    link(pool.tensor_tensor(y, y, s, ALU.mult))
                pool.sem_inc(pair_norm, 2)

            with pool.Fori(0, B // 2) as j:
                pair_norms(j, 0)

            pool.wait_ge(x_maxed, 1)
            pool.partition_all_reduce(x_allmax[:, :], x_max[:, :], 128, RMAX).then_inc(x_alled, 1)
            with pool.Fori(0, B // 2) as j:
                pair_norms(j, 1)

            pool.wait_ge(added1, B)
            pool.memset(lower[:, :], 1.0)
            pool.memset(ones[:, :], 1.0)
            pool.memset(valid[:, :], 1.0)
            pool.memset(carry[:, :, :], 1.0)
            pool.iota(iota_e[:, :], pattern=[[1, EXPERTS]], base=-EXPERTS, channel_multiplier=0,
                      allow_small_or_imprecise_dtypes=True)
            pool.iota(iota_t[:, :], pattern=[[1, XT]], base=0, channel_multiplier=0,
                      allow_small_or_imprecise_dtypes=True).then_inc(e_consts, 1)
            pool.wait_ge(e_consts, 2)
            pool.affine_select(out=lower[:, :], in_=lower[:, :], compare_op=ALU.is_gt, fill=0.0,
                               base=0, pattern=[[1, 128]], channel_multiplier=-1)
            pool.affine_select(out=valid[:, 1::2], in_=valid[:, 1::2], compare_op=ALU.is_ge, fill=0.0,
                               base=TB - 1, pattern=[[0, B]], channel_multiplier=-1)
            pool.memset(carry[:, :, 0:1], 0.0).then_inc(e_consts, 1)
            pool.wait_ge(e_consts, 3)
            for turned_x in (exT, ehT):
                for n in range(2):
                    ins = pool.memset(turned_x[n][1][DB:DB + 1, :], 1.0)
            ins.then_inc(e_consts, 1)

            pool.wait_ge(slots_ready, 1)
            pool.wait_ge(e_zeroed, 16)
            for k in range(2 * B):
                rows = TILES[k % 2][1]
                pool.indirect_dma_start(xs_dram[:, :], bass.IndirectOffsetOnAxis(ap=slot_i[0:rows, k:k + 1], axis=0),
                                        xn4[0:rows, k, :], None).then_inc(sent, 16)
            pool.wait_ge(sent, 16 * 2 * B)
            for n in range(4):
                pool.wait_ge(ys_stored[n], 16 * len(range(n, XT, 4)))
            for k in range(2 * B):
                rows = TILES[k % 2][1]
                need(pool, summed, k // 2 - 3)
                pool.indirect_dma_start(xn4[0:rows, k, :], None, ys_dram[:, :],
                                        bass.IndirectOffsetOnAxis(ap=slot_i[0:rows, k:k + 1], axis=0)).then_inc(back[k // 2 % 4], 16)


        @block.scalar
        def _(act):
            sd = small_loaded
            act.dma_start(tok_w[:, :], I["L0_tok_w"].rearrange("d o -> (d o)").partition_broadcast(128)).then_inc(sd, 16)
            act.dma_start(tok_b[:, :], I["L0_tok_b"].partition_broadcast(128)).then_inc(sd, 16)
            act.dma_start(bs_neg[:, :], I["L0_attn_bs"].partition_broadcast(128)).then_inc(sd, 16)
            for h in range(8):
                act.dma_start(ws_col[HD * h:HD * h + HD, :], I["L0_attn_ws"].rearrange("(d o) -> d o", o=1)).then_inc(sd, 16)
            w = w0_loaded
            for dst, wt, bias in ((wq0, "L0_attn_WqT", "L0_attn_bq"), (wk0, "L0_attn_WkT", "L0_attn_bk")):
                for r, (lo, hi) in enumerate(((0, DA), (DA, D))):
                    act.dma_start(dst[r][0:hi - lo, 0:D], I[wt][lo:hi, :]).then_inc(w, 16)
                    act.dma_start(dst[r][0:hi - lo, D:256], I[wt][lo:hi, DA:D]).then_inc(w, 16)
                row = I[bias].rearrange("(o d) -> o d", o=1)
                act.dma_start(dst[1][DB:DB + 1, 0:D], row).then_inc(w, 16)
                act.dma_start(dst[1][DB:DB + 1, D:256], row[:, DA:D]).then_inc(w, 16)
            for dst, wt, bias in ((wv0, "L0_attn_WvT", "L0_attn_bv"), (wo0, "L0_attn_WoT", "L0_attn_bo")):
                act.dma_start(dst[0][:, :], I[wt][0:DA, :]).then_inc(w, 16)
                act.dma_start(dst[1][0:DB, :], I[wt][DA:D, :]).then_inc(w, 16)
                act.dma_start(dst[1][DB:DB + 1, :], I[bias].rearrange("(o d) -> o d", o=1)).then_inc(w, 16)

            act.preload_act_table_set("exp_and_others")
            act.wait_ge(filled, 1)
            act.sem_inc(resid_ready, 2)
            with act.Fori(0, B // 2) as i:
                for par in range(2):
                    b = 2 * i + par
                    act.wait_ge(picked, b + 3)
                    for t, rows in TILES:
                        ins = act.activation(resid[0:rows, b + 1, t, :], bank_k[par][0:rows, t * D:(t + 1) * D], ACT.Copy)
                    ins.then_inc(resid_ready, 1)
            act.wait_ge(var_ready, 1)
            act.activation(std[:, :], var[:, :], ACT.Sqrt).then_inc(std_ready, 1)

            act.preload_act_table_set("exp_and_others")
            act.sem_inc(exp_done, 2)

            def exps(n, slot):
                act.wait_ge(smax_done, n + 1)
                act.wait_ge(turned, n + 1)
                act.activation(p_sb[slot][:, :], s_sb[slot][:, :], ACT.Exp, bias=s_min[slot][:, :],
                               scale=-1.0).then_inc(exp_done, 1)

            with act.Fori(0, B // 2) as i:
                for par in range(2):
                    for g in range(GROUPS):
                        n = i * BODY + par * GROUPS + g
                        slot = (par * GROUPS + g) % 2
                        act.wait_ge(args_dve, n + 1)
                        act.wait_ge(args_pool, n + 1)
                        w = units(g) * KEEP
                        a = arg_slot(par * GROUPS + g)[0][:, 0:w]
                        act.activation(a, a, ACT.Tanh).then_inc(tanh_done, 1)
                        exps(n, slot)
            for n in range(B * GROUPS, B * GROUPS + 2):
                exps(n, n % 2)

            act.wait_ge(var_ready, 2)
            act.activation(std[:, :], var[:, :], ACT.Sqrt).then_inc(std_ready, 1)
            act.preload_act_table(ACT.Gelu)

            def ffn_step(i, par):
                if real(i + 1):
                    act.wait_ge(f_xT_psum, i + 2)
                    if not isinstance(i, int) or i >= 1:
                        act.wait_ge(h_psum, HT // 2 * i)
                    x = fx[1 - par]
                    act.activation(x[0][:, :], bank_pre[:, 0:KEEP], ACT.Copy)
                    act.activation(x[1][:, :], bank_pre[0:DB, KEEP:2 * KEEP], ACT.Copy).then_inc(f_xT_ready, 1)
                if real(i):
                    if not isinstance(i, int) or i >= 2:
                        act.wait_ge(hq_ready, i - 1)
                    for c in range(HT):
                        if c % 2 == 0:
                            act.wait_ge(h_psum, HT // 2 * i + c // 2 + 1)
                        ins = act.activation(gelu[par][:, c * KEEP:(c + 1) * KEEP],
                                             ffn_banks[par][c // 2][:, c % 2 * KEEP:(c % 2 + 1) * KEEP],
                                             ACT.Gelu, bias=b1_col[:, c:c + 1], scale=w_scale[:, 0:1])
                    ins.then_inc(gelu_done, 1)

            ffn_step(-1, 1)
            staged(act, ffn_step, (1, 0))

            act.preload_act_table_set("exp_and_others")

            def attn1_step(b, par):
                for u in range(PAIRS):
                    n, slot = PAIRS * b + u, u % 2
                    m = n - 2
                    if real(m, PAIRS * B):
                        uu, pp = ((u - 2), par) if u >= 2 else (u - 2 + PAIRS, 1 - par)
                        act.wait_ge(pair_turned, m + 1)
                        cols = slice(2 * uu * KEEP, 2 * uu * KEEP + 2 * KEEP)
                        act.activation(pt1[pp][0][:, cols], bank_pt[0][:, 0:2 * KEEP], ACT.Copy)
                        act.activation(pt1[pp][1][0:TB, cols], bank_pt[1][0:TB, 0:2 * KEEP], ACT.Copy).then_inc(pair_pt, 1)
                    if real(n, PAIRS * B):
                        act.wait_ge(pair_neg, n + 1)
                        need(act, pair_clipped, n - 1)
                        for e in range(2):
                            for t in range(2):
                                c = 2 * e + t
                                ins = act.activation(y1[slot][:, c * KEEP:(c + 1) * KEEP], pair_banks[slot][:, e, t, :],
                                                     ACT.Identity, bias=pneg[slot][:, c:c + 1], scale=C2 * 2.0 ** 23)
                        ins.then_inc(pair_scaled, 1)
                    if u == 0 and real(b - 1):
                        ctx1_part(b - 1, 0, 2, 0)
                    if u == 2 and real(b - 1):
                        ctx1_part(b - 1, 2, 3, 1)
                    if u == 4 and real(b - 1):
                        act.wait_ge(ctx1T_psum, b)
                        act.activation(ctxT[0][:, :], bank_out[:, 0:KEEP], ACT.Copy)
                        act.activation(ctxT[1][0:DB, :], bank_out[0:DB, KEEP:2 * KEEP], ACT.Copy).then_inc(ctx1T_ready, 1)
                    if u == 0 and real(b - 5):
                        act.wait_ge(gxT_psum, b - 4)
                        need(act, gate_psum, b - 5)
                        act.activation(xT[0][:, :], bank_pre[:, 0:KEEP], ACT.Copy)
                        act.activation(xT[1][0:DB, :], bank_pre[0:DB, KEEP:2 * KEEP], ACT.Copy).then_inc(gxT_ready, 1)
                    if u == 1 and real(b + 1):
                        xqT_out(b + 1, 1 - par)
                    if u == 3 and real(b + 1):
                        k_out(b + 1, 1 - par)

            def ctx1_part(b, lo, hi, k):
                act.wait_ge(ctx1_psum, 2 * b + k + 1)
                act.activation(ctx1[:, lo * KEEP:hi * KEEP], bank_out[:, 0:(hi - lo) * KEEP], ACT.Copy).then_inc(ctx1_out, 1)

            def xqT_out(c, par):
                act.wait_ge(xqT_psum, c + 1)
                b16 = bank_pre.bitcast(BF16)
                act.activation(xqT[par][0][:, :], b16[:, 0:KEEP], ACT.Copy)
                act.activation(xqT[par][1][:, :], b16[0:DB, 256:256 + KEEP], ACT.Copy).then_inc(xqT_ready, 1)

            def k_out(c, par):
                act.wait_ge(qkv_psum, 4 * c + 2)
                for r in range(2):
                    ins = act.activation(k1[par][:, r, :], bank_pre[:, r * KEEP:(r + 1) * KEEP],
                                         ACT.Identity, bias=bqk1[1][:, r:r + 1], scale=x_scale[:, :])
                ins.then_inc(qkv_out, 1)

            act.wait_ge(x3_step, 2)
            xqT_out(0, 0)
            k_out(0, 0)
            staged(act, attn1_step, (1, 5))

            act.preload_act_table(ACT.Gelu)
            act.wait_ge(e_consts, 4)

            def expert_step(i, par):
                if real(i, XT):
                    x = exT[par % 2]
                    act.wait_ge(exT_psum, i + 1)
                    need(act, eh_psum, i - 1)
                    act.activation(x[0][:, :], bank_k[par % 2][:, 0:128], ACT.Copy)
                    act.activation(x[1][0:DB, :], bank_k[par % 2][0:DB, 128:256], ACT.Copy).then_inc(exT_ready, 1)
                if real(i - 1, XT):
                    slot = (par + 1) % 2
                    act.wait_ge(eh_psum, i)
                    need(act, ehT_psum, i - 2)
                    act.activation(eh[slot][:, :], bank_s[slot][:, 0:D], ACT.Gelu).then_inc(eh_ready, 1)
                if real(i - 3, XT):
                    slot = (par + 1) % 4
                    act.wait_ge(ey_psum, i - 2)
                    if real(i - 7, XT):
                        act.wait_ge(ys_stored[slot], 4 * (i - 7 - slot) + 16)
                    act.activation(ey[slot][:, :], out_banks[slot % 2][:, 0:D], ACT.Copy).then_inc(ey_ready, 1)
                if real(i - 4, XT):
                    act.wait_ge(ey_ready, i - 3)
                    act.dma_start(ys_dram[bass.ds(128 * (i - 4), 128), :], ey[par][:, :]).then_inc(ys_stored[par], 16)

            staged(act, expert_step, (0, 8), XT, 4)

        @block.vector
        def _(dve):
            for part in (tstats[:, :, :], resid[:, 0, :, :], resid[:, SLOTS - 1, :, :], stats[:, :, :], mean[:, :], rstd[:, :],
                         q_cols[0][:, :], q_cols[1][:, :], v_sb[0][:, :, :, :], v_sb[1][:, :, :, :],
                         xT[1][DB:DB + 1, :], ctxT[1][DB:DB + 1, :],
                         bank_s[0][:, :], bank_s[1][:, :], bank_pt[0][:, :], bank_pt[1][:, :], p_sb[0][:, :], p_sb[1][:, :]):
                ins = dve.memset(part, 1.0)
            ins.then_inc(filled, 1)
            dve.wait_ge(filled, 1)
            logits, hot, work_a, work_b = gate
            dve.memset(logits, 0.0).then_inc(g_step, 1)
            dve.sem_inc(norm_used, 2)

            dve.wait_ge(small_loaded, 16 * 11)
            dve.wait_ge(x_loaded, 16 * 4)
            for k in range(2 * B):
                ins = dve.tensor_tensor_reduce(x_prod[:, k, :], x_all[:, k, :], tok_w[:, :], 1.0, 0.0,
                                               ALU.mult, ALU.add, tok_score[:, k:k + 1])
            ins.then_inc(dots_done, 1)
            dve.wait_ge(dots_done, 1)
            dve.tensor_scalar(tok_score[:, :], tok_score[:, :], tok_b[:, :], None, ALU.add).then_inc(scores_ready, 1)
            dve.wait_ge(consts, 1)
            dve.tensor_scalar(ws_place[:, :, :], ws_place[:, :, :], ws_col[:, :], -1.0, ALU.mult, ALU.mult).then_inc(ws_ready, 1)
            dve.tensor_scalar(bs_neg[:, :], bs_neg[:, :], -1.0, None, ALU.mult).then_inc(ws_ready, 1)
            dve.wait_ge(ws_ready, 2)
            dve.wait_ge(scoresT_psum, 1)
            dve.tensor_copy(tok_rowsT[:, :], bank_out[0:2 * B, 0:128]).then_inc(scoresT_ready, 1)

            dve.wait_ge(wf_loaded, 16 * 7)
            wlink = [0]

            def wchain(ins):
                wlink[0] += 1
                ins.then_inc(w_step, 1)
                dve.wait_ge(w_step, wlink[0])

            wchain(dve.memset(w_max[:, :], 0.0))
            dve.tensor_reduce(w_max[:, 0:1], w1q[0][:, :], AX.X, ALU.max, apply_absolute_value=True)
            wchain(dve.tensor_reduce(w_max[:, 2:3], w2f[:, :, :], AX.XY, ALU.max, apply_absolute_value=True))
            wchain(dve.tensor_reduce(w_max[0:DB, 1:2], w1q[1][:, :], AX.X, ALU.max, apply_absolute_value=True))
            dve.tensor_tensor(w_maxes[:, 0:1], w_max[:, 0:1], w_max[:, 1:2], ALU.max)
            dve.tensor_copy(w_maxes[:, 1:2], w_max[:, 2:3]).then_inc(w_maxed, 1)
            dve.reciprocal(inv_gelu[:, :], s_gelu[:, :])
            wchain(dve.reciprocal(inv_out[:, :], s_out[:, :]))
            dve.wait_ge(w_alled, 1)
            wchain(dve.tensor_scalar(w_scale[:, :], w_all[:, :], 1.0 / 127.0, None, ALU.mult))
            wchain(dve.reciprocal(w_inv[:, :], w_scale[:, :]))
            wchain(dve.tensor_tensor(y_scale[:, :], s_gelu[:, :], w_scale[:, 1:2], ALU.mult))
            dve.tensor_tensor(y_scale[:, :], y_scale[:, :], inv_out[:, :], ALU.mult)
            wchain(dve.tensor_scalar(b2_row[:, :], b2_row[:, :], inv_out[:, :], None, ALU.mult))
            dve.sem_inc(w_scaled, 1)

            def tile_stats(slot):
                for t, rows in TILES:
                    ins = dve.bn_stats(stats[0:rows, 2 * slot + t, :], resid[0:rows, slot, t, :])
                return ins

            def pick_step(i, par):
                if real(i):
                    for t in range(2):
                        k = 2 * i + t
                        row = score_rows[:, bass.ds(i * N, N)]
                        me = tok_score[:, bass.ds(k, 1)]
                        dve.tensor_scalar(cmp_junk[4 * par + 2 * t][:, 0:N], row, me, None, ALU.is_gt, ALU.add,
                                          accum_out=above[:, bass.ds(k, 1)])
                        ins = dve.scalar_tensor_tensor(cmp_junk[4 * par + 2 * t + 1][:, 0:N], row, me, earlier[:, t, :],
                                                       ALU.is_equal, ALU.mult, accum_out=ties[:, bass.ds(k, 1)])
                    ins.then_inc(compared, 1)
                    dve.wait_ge(compared, i + 1)
                    dve.tensor_tensor(rank[:, bass.ds(2 * i, 2)], above[:, bass.ds(2 * i, 2)], ties[:, bass.ds(2 * i, 2)],
                                      ALU.add).then_inc(rank_ready, 1)
                if real(i - 3):
                    dve.wait_ge(resid_ready, i)
                    tile_stats(i - 2).then_inc(stats_done, 1)
                if real(i):
                    dve.wait_ge(picked, i + 1)
                    dve.wait_ge(rank_ready, i + 1)
                    for t in range(2):
                        ins = dve.tensor_scalar(onehot[:, par % 2, t, :], iota_keep[:, :], rank[:, bass.ds(2 * i + t, 1)],
                                                None, ALU.is_equal)
                    ins.then_inc(onehot_ready, 1)

            dve.wait_ge(rows_loaded, 16 * 4)
            staged(dve, pick_step, (0, 3), B, 4)

            steps = [0]

            def link(ins):
                steps[0] += 1
                ins.then_inc(ln_step, 1)
                dve.wait_ge(ln_step, steps[0])

            def finish_stats(n):
                mE, mO, vE, vO = (stats[:, :, c] for c in (1, 4, 2, 5))
                dve.tensor_tensor(mean[:, :], mE, mO, ALU.add)
                dve.tensor_tensor(diff[:, :], mE, mO, ALU.subtract)
                link(dve.tensor_tensor(var[:, :], vE, vO, ALU.add))
                dve.tensor_scalar(mean[:, :], mean[:, :], 0.5, None, ALU.mult)
                dve.tensor_scalar(var[:, :], var[:, :], 1.0 / D, EPS, ALU.mult, ALU.add)
                link(dve.scalar_tensor_tensor(diff[:, :], diff[:, :], 0.25, diff[:, :], ALU.mult, ALU.mult))
                dve.tensor_tensor(var[:, :], var[:, :], diff[:, :], ALU.add).then_inc(var_ready, 1)
                dve.wait_ge(std_ready, n)
                link(dve.reciprocal(rstd[:, :], std[:, :]))
                link(dve.tensor_tensor(newt[:, :], rstd[:, :], rstd[:, :], ALU.mult))
                link(dve.tensor_tensor(newt[:, :], newt[:, :], var[:, :], ALU.mult))
                link(dve.tensor_scalar(newt[:, :], newt[:, :], -0.5, 1.5, ALU.mult, ALU.add))
                link(dve.tensor_tensor(rstd[:, :], rstd[:, :], newt[:, :], ALU.mult))

            dve.wait_ge(stats_done, B)
            finish_stats(1)

            def normalise(slot):
                for t, rows in TILES:
                    k = 2 * slot + t
                    ins = dve.tensor_scalar(normed[0:rows, t, :], resid[0:rows, slot, t, :],
                                            mean[0:rows, bass.ds(k, 1)], rstd[0:rows, bass.ds(k, 1)],
                                            ALU.subtract, ALU.mult)
                return ins

            def pre_norm(c):
                normalise(c + 1).then_inc(normed_ready, 1)

            def pre_xT(c):
                dve.wait_ge(xT_psum, c + 1)
                dve.tensor_copy(xT[0][:, :], bank_pre[:, 0:KEEP])
                dve.tensor_copy(xT[1][0:DB, :], bank_pre[0:DB, KEEP:2 * KEEP]).then_inc(xT_ready, 1)

            def pre_q(c, par):
                dve.wait_ge(q_psum, c + 1)
                q = q_cols[par]
                dve.tensor_copy(q[:, 0:UA], bank_pre[:, 0:KEEP])
                dve.tensor_copy(q[0:64, UA:UNITS], bank_pre[0:64, KEEP:2 * KEEP:2])
                dve.tensor_copy(q[64:128, UA:UNITS - 1], bank_pre[64:128, KEEP + 1:2 * KEEP:2]).then_inc(q_ready, 1)

            def pre_k(c, par):
                dve.wait_ge(k_psum, c + 1)
                dve.tensor_copy(k_sb[par][:, :], bank_k[par][:, 0:2 * KEEP]).then_inc(k_ready, 1)

            def pre_v(c, par):
                dve.wait_ge(v_psum, c + 1)
                for t, rows in TILES:
                    ins = dve.tensor_copy(v_sb[par][0:rows, t, :, 0:HD],
                                          bank_pre[0:rows, t * D:(t + 1) * D].rearrange("p (h d) -> p h d", d=HD))
                ins.then_inc(v_ready, 1)

            def turn_out(b, par, c):
                last = min(CHUNK * c + CHUNK, GROUPS) - 1
                cols = (last + 1 - CHUNK * c) * 128
                dve.wait_ge(turned, b * GROUPS + last + 5)
                dve.tensor_copy(pt[par][0][:, CHUNK * c * 128:CHUNK * c * 128 + cols], bank_pt[0][:, 0:cols])
                dve.tensor_copy(pt[par][1][0:TB, CHUNK * c * 128:CHUNK * c * 128 + cols],
                                bank_pt[1][0:TB, 0:cols]).then_inc(pt_ready, 1)

            def ctx_out(b):
                dve.wait_ge(ctx_psum, b + 1)
                for t, rows in TILES:
                    c = bank_out[0:rows, t * HEADS * VC:(t + 1) * HEADS * VC].rearrange("p (h v) -> p h v", v=VC)
                    ins = dve.reciprocal(inv_sum[0:rows, t, :], c[:, :, HD])
                ins.then_inc(ctx_inv, 1)
                dve.wait_ge(ctx_inv, b + 1)
                for t, rows in TILES:
                    c = bank_out[0:rows, t * HEADS * VC:(t + 1) * HEADS * VC].rearrange("p (h v) -> p h v", v=VC)
                    ins = dve.tensor_tensor(ctx_sb[0:rows, t, :].rearrange("p (h d) -> p h d", d=HD), c[:, :, 0:HD],
                                            inv_sum[0:rows, t, :].unsqueeze(2).to_broadcast([rows, HEADS, HD]), ALU.mult)
                ins.then_inc(ctx_ready, 1)

            def ctxT_out(b):
                dve.wait_ge(ctxT_psum, b + 1)
                dve.tensor_copy(ctxT[0][:, :], bank_out[:, 0:KEEP])
                dve.tensor_copy(ctxT[1][0:DB, :], bank_out[0:DB, KEEP:2 * KEEP]).then_inc(ctxT_ready, 1)

            def add_out(b):
                dve.wait_ge(proj_psum, b + 1)
                for t, rows in TILES:
                    ins = dve.tensor_tensor(resid[0:rows, b, t, :], resid[0:rows, b, t, :],
                                            bank_out[0:rows, t * D:(t + 1) * D], ALU.add)
                ins.then_inc(resid_added, 1)
                dve.wait_ge(resid_added, 2 * b + 1)
                tile_stats(b).then_inc(resid_added, 1)

            def dve_sums(b, par, g):
                n = b * GROUPS + g
                if g == 0:
                    dve.wait_ge(q_ready, b + 1)
                slot, back_to = arg_slot(par * GROUPS + g)
                dve.wait_ge(scored, n + 3 - back_to)
                sums(dve, slot, bank_k[par], q_cols[par], g, 0, DVE_UNITS).then_inc(args_dve, 1)

            def smax(b, par, g):
                n = b * GROUPS + g
                slot = (par * GROUPS + g) % 2
                dve.wait_ge(scored, n + 1)
                dve.wait_ge(exp_done, n + 1)
                dve.tensor_scalar(s_sb[slot][:, :], bank_s[slot][:, 0:KEEP], bs_neg[:, :], None, ALU.add, ALU.min,
                                  accum_out=s_min[slot][:, :]).then_inc(smax_done, 1)

            def lagging(b, par, g, last=False):
                if g == 3:
                    turn_out(b - 1, 1 - par, 3)
                if g == 4:
                    turn_out(b - 1, 1 - par, 4)
                if g == 11:
                    ctx_out(b)
                if g == 13:
                    ctxT_out(b)
                if g == 15:
                    add_out(b)
                if last:
                    return
                if g in (8, 12, 16):
                    turn_out(b, par, g // 4 - 2)
                if g == 0:
                    pre_norm(b + 1)
                if g == 5:
                    pre_xT(b + 1)
                if g == 12:
                    pre_q(b + 1, 1 - par)
                if g == 14:
                    pre_k(b + 1, 1 - par)
                if g == 16:
                    pre_v(b + 1, 1 - par)

            dve.memset(pt[1][0], 1.0)
            dve.memset(pt[1][1][0:TB, :], 1.0)
            pre_norm(0)
            pre_xT(0)
            pre_q(0, 0)
            pre_k(0, 0)
            pre_v(0, 0)
            with dve.Fori(0, B // 2) as i:
                for par in range(2):
                    b = 2 * i + par
                    for g in range(GROUPS):
                        dve_sums(b, par, g)
                        smax(b, par, g)
                        lagging(b, par, g)
            for g in range(GROUPS):
                if g < 2:
                    smax(B, 0, g)
                lagging(B, 0, g, last=True)

            dve.wait_ge(resid_added, 2 * (B + 1))
            finish_stats(2)

            def ffn_norm(i, par):
                for t, rows in TILES:
                    k = 2 * (i + 1) + t
                    ins = dve.tensor_scalar(fnorm[par][0:rows, t, :], resid[0:rows, i + 1, t, :],
                                            mean[0:rows, bass.ds(k, 1)], rstd[0:rows, bass.ds(k, 1)],
                                            ALU.subtract, ALU.mult)
                ins.then_inc(f_normed, 1)

            def ffn_step(i, par):
                if real(i + 2):
                    dve.wait_ge(f_xT_psum, i + 1)
                    ffn_norm(i + 2, par)
                if real(i - 2):
                    b = i - 2
                    dve.wait_ge(y_psum, b + 1)
                    n = 3 * b
                    for t, rows in TILES:
                        ins = dve.scalar_tensor_tensor(y_sb[0:rows, t, :], bank_out[0:rows, t * D:(t + 1) * D],
                                                       y_scale[0:rows, :], b2_row[0:rows, :], ALU.mult, ALU.add)
                    ins.then_inc(y_step, 1)
                    dve.wait_ge(y_step, n + 1)
                    for t, rows in TILES:
                        ins = dve.tensor_scalar(y_sb[0:rows, t, :], y_sb[0:rows, t, :], -128.0, 127.0, ALU.max, ALU.min)
                    ins.then_inc(y_step, 1)
                    dve.wait_ge(y_step, n + 2)
                    for t, rows in TILES:
                        ins = dve.tensor_scalar(y_sb[0:rows, t, :], y_sb[0:rows, t, :], MAGIC, MAGIC, ALU.add, ALU.subtract)
                    ins.then_inc(y_step, 1)
                    dve.wait_ge(y_step, n + 3)
                    for t, rows in TILES:
                        r = resid[0:rows, b + 1, t, :]
                        ins = dve.scalar_tensor_tensor(r, y_sb[0:rows, t, :], s_out[0:rows, :], r, ALU.mult, ALU.add)
                    ins.then_inc(f_added, 1)
                if real(i - 1):
                    b = i - 1
                    g, q = gelu[1 - par], hq[1 - par]
                    dve.wait_ge(gelu_done, b + 1)
                    dve.tensor_scalar(g, g, inv_gelu[:, :], -128.0, ALU.mult, ALU.max).then_inc(quant_step, 1)
                    dve.wait_ge(quant_step, 2 * b + 1)
                    dve.tensor_scalar(g, g, 127.0, MAGIC, ALU.min, ALU.add).then_inc(quant_step, 1)
                    dve.wait_ge(quant_step, 2 * b + 2)
                    if not isinstance(b, int) or b >= 2:
                        dve.wait_ge(y_psum, b - 1)
                    dve.tensor_scalar(q, g, MAGIC, None, ALU.subtract).then_inc(hq_ready, 1)
                if real(i - 2):
                    dve.wait_ge(f_added, i - 1)
                    need(dve, stats_taken, i - 2 - par)
                if real(i - 5):
                    norm_max(i - 5, 1 - par)
                if real(i - 2):
                    pair_tile_stats(i - 1, par)

            def pair_tile_stats(slot, par):
                for t, rows in TILES:
                    ins = dve.bn_stats(tstats[0:rows, 2 * par + t, :], resid[0:rows, slot, t, :])
                ins.then_inc(pair_stats, 1)

            def norm_max(b, par):
                dve.wait_ge(pair_norm, b - par + 2)
                for t, rows in TILES:
                    k = 2 * par + t
                    ins = dve.tensor_scalar(xn3[0:rows, bass.ds(2 * b + t, 1), :].rearrange("p o d -> p (o d)"),
                                            resid[0:rows, b + 1, t, :], tmean[0:rows, k:k + 1], trstd[0:rows, k:k + 1],
                                            ALU.subtract, ALU.mult)
                ins.then_inc(norm_used, 1)
                dve.wait_ge(norm_used, b + 3)
                for t, rows in TILES:
                    ins = dve.tensor_reduce(mx3[0:rows, bass.ds(2 * b + t, 1)],
                                            xn3[0:rows, bass.ds(2 * b + t, 1), :].rearrange("p o d -> p (o d)"),
                                            AX.X, ALU.max, apply_absolute_value=True)
                ins.then_inc(n3_step, 1)

            ffn_norm(0, 0)
            ffn_norm(1, 1)
            dve.wait_ge(w1_step, 3)
            staged(dve, ffn_step, (2, 5))

            dve.wait_ge(qv_blank, 4)
            dve.wait_ge(n3_step, B)
            dve.tensor_reduce(x_max[:, :], mx3[:, :], AX.X, ALU.max).then_inc(x_maxed, 1)
            dve.wait_ge(x_alled, 1)
            dve.tensor_scalar(x_scale[:, :], x_allmax[:, :], 1.0 / 127.0, 1e-8, ALU.mult, ALU.max).then_inc(x3_step, 1)
            dve.wait_ge(x3_step, 1)
            dve.reciprocal(x_inv[:, :], x_scale[:, :]).then_inc(x3_step, 1)
            dve.wait_ge(x3_step, 2)
            def xq_make(c, par, step):
                if step == 2:
                    need(dve, xqT_psum, c - 1)
                if step:
                    dve.wait_ge(xq_step, 2 * c + step)
                for t, rows in TILES:
                    x = xn3[0:rows, bass.ds(2 * c + t, 1), :].rearrange("p o d -> p (o d)")
                    if step == 0:
                        ins = dve.tensor_scalar(x, x, x_inv[0:rows, :], -128.0, ALU.mult, ALU.max)
                    if step == 1:
                        ins = dve.tensor_scalar(x, x, 127.0, MAGIC, ALU.min, ALU.add)
                    if step == 2:
                        ins = dve.tensor_scalar(xq[par][0:rows, t, :], x, MAGIC, None, ALU.subtract)
                ins.then_inc(xq_step if step < 2 else xq_ready, 1)

            def q_out(c, par, fill):
                dve.wait_ge(qkv_psum, 4 * c + fill + 1)
                for col in range(2):
                    src = bank_pre[:, col * KEEP:(col + 1) * KEEP]
                    kind, r = (0, col) if fill == 0 else (col, 2)
                    dst = (q1 if kind == 0 else k1)[par][:, r, 0:KEEP]
                    ins = dve.tensor_scalar(dst, src, x_scale[:, :], bqk1[kind][:, r:r + 1], ALU.mult, ALU.add)
                ins.then_inc(qkv_out, 1)

            def v_out(c, par):
                dve.wait_ge(qkv_psum, 4 * c + 4)
                for t, rows in TILES:
                    ins = dve.scalar_tensor_tensor(
                        v1[par][0:rows, t, :, 0:HD],
                        bank_pre[0:rows, t * D:(t + 1) * D].rearrange("p (h d) -> p h d", d=HD), x_scale[0:rows, :],
                        bv1[0:rows, :].rearrange("p (h d) -> p h d", d=HD), ALU.mult, ALU.add)
                ins.then_inc(qkv_out, 1)

            def ctx1_divide(b, lo, hi, k):
                n = hi - lo
                dve.wait_ge(ctx1_tokens, 2 * b + k + 1)
                for t, rows in TILES:
                    c = bank_out[0:rows, t * 128 * n:(t + 1) * 128 * n].rearrange("p (h v) -> p h v", v=32)
                    ins = dve.reciprocal(inv_sum[0:rows, t, 4 * lo:4 * hi], c[:, :, HD])
                ins.then_inc(ctx1_inv, 1)
                dve.wait_ge(ctx1_inv, 2 * b + k + 1)
                for t, rows in TILES:
                    c = bank_out[0:rows, t * 128 * n:(t + 1) * 128 * n].rearrange("p (h v) -> p h v", v=32)
                    ins = dve.tensor_tensor(
                        ctx_sb[0:rows, t, 4 * lo * HD:4 * hi * HD].rearrange("p (h d) -> p h d", d=HD), c[:, :, 0:HD],
                        inv_sum[0:rows, t, 4 * lo:4 * hi].unsqueeze(2).to_broadcast([rows, 4 * n, HD]), ALU.mult)
                ins.then_inc(ctx1_ready, 1)

            def attn1_step(b, par):
                for u in range(PAIRS):
                    n, slot = PAIRS * b + u, u % 2
                    if u == 0 and real(b - 2):
                        dve.wait_ge(proj1_psum, b - 1)
                        for t, rows in TILES:
                            r = resid[0:rows, b - 1, t, :]
                            ins = dve.tensor_tensor(r, r, bank_out[0:rows, t * D:(t + 1) * D], ALU.add)
                        ins.then_inc(added1, 1)
                    if real(n, PAIRS * B):
                        dve.wait_ge(pair_scored, n + 1)
                        need(dve, pair_scaled, n - 1)
                        dve.tensor_reduce(pmax[slot][:, :, :], pair_banks[slot], AX.X, ALU.max).then_inc(pair_maxed, 1)
                    if u == 2 and real(b - 5):
                        dve.wait_ge(gate_psum, b - 4)
                        for t, rows in TILES:
                            ins = dve.tensor_copy(
                                logits[0:rows, :, bass.ds(2 * (b - 5) + t, 1)].rearrange("p e o -> p (e o)"),
                                bank_k0[0:rows, 2 * KEEP + t * EXPERTS:2 * KEEP + (t + 1) * EXPERTS])
                        ins.then_inc(gate_out, 1)
                    if real(n, PAIRS * B):
                        dve.wait_ge(pair_maxed, n + 1)
                        dve.tensor_scalar(pneg[slot][:, :], pmax[slot][:, :, :].rearrange("p e t -> p (e t)"),
                                          -C2 * 2.0 ** 23, None, ALU.mult).then_inc(pair_neg, 1)
                    if real(n - 1, PAIRS * B):
                        other = p1[1 - slot].bitcast(I32)
                        dve.wait_ge(pair_scaled, n)
                        need(dve, pair_turned, n - 2)
                        dve.tensor_scalar(other, y1[1 - slot], -1.0, -126.0 * 2.0 ** 23, ALU.min, ALU.max).then_inc(pair_clipped, 1)
                        dve.wait_ge(pair_clipped, n)
                        dve.tensor_scalar(other, other, -(1 << 30), None, ALU.bitwise_xor).then_inc(pair_powered, 1)
                    if u == 1 and real(b - 1):
                        ctx1_divide(b - 1, 0, 2, 0)
                    if u == 3 and real(b - 1):
                        ctx1_divide(b - 1, 2, 3, 1)
                    if u == 2 and real(b - 2):
                        dve.wait_ge(added1, b - 1)
                    if u == 2 and real(b - 4):
                        norm4(b - 4, par)
                    if u == 2 and real(b - 2):
                        pair_tile_stats(b - 1, par)
                    if u >= 3 and real(b + 2):
                        xq_make(b + 2, par, u - 3)
                    if not real(b + 1):
                        continue
                    if u in (2, 4):
                        q_out(b + 1, 1 - par, u - 2)
                    if u == 5:
                        v_out(b + 1, 1 - par)

            def norm4(b, par):
                dve.wait_ge(pair_norm, B + b - par + 2)
                need(dve, gxT_psum, b - 1)
                for t, rows in TILES:
                    k = 2 * par + t
                    ins = dve.tensor_scalar(fnorm[par][0:rows, t, :], resid[0:rows, b + 1, t, :],
                                            tmean[0:rows, k:k + 1], trstd[0:rows, k:k + 1], ALU.subtract, ALU.mult)
                ins.then_inc(norm_used, 1)
                dve.wait_ge(norm_used, B + b + 3)
                for t, rows in TILES:
                    ins = dve.tensor_copy(xn4[0:rows, bass.ds(2 * b + t, 1), :].rearrange("p o d -> p (o d)"),
                                          fnorm[par][0:rows, t, :])
                ins.then_inc(n4_ready, 1)

            for c in range(2):
                for step in range(3):
                    xq_make(c, c, step)
            q_out(0, 0, 0)
            q_out(0, 0, 2)
            v_out(0, 0)
            staged(dve, attn1_step, (2, 5))

            dve.wait_ge(e_consts, 4)
            gsteps = [1]

            def glink(ins):
                gsteps[0] += 1
                ins.then_inc(g_step, 1)
                dve.wait_ge(g_step, gsteps[0])

            ek = [128, EXPERTS, 2 * B]
            by_token = "p e k -> p k e"
            over_k = lambda a: a[:, :].unsqueeze(2).to_broadcast(ek)
            over_e = lambda a: a[:, :].unsqueeze(1).to_broadcast(ek)
            dve.wait_ge(gate_out, B)
            glink(dve.tensor_reduce(top[:, :], logits.rearrange(by_token), AX.X, ALU.max))
            glink(dve.tensor_tensor(hot, logits, over_e(top), ALU.is_ge))
            glink(dve.tensor_tensor(hot, hot, over_k(iota_e), ALU.mult))
            glink(dve.tensor_reduce(top[:, :], hot.rearrange(by_token), AX.X, ALU.min))
            glink(dve.tensor_tensor(hot, over_k(iota_e), over_e(top), ALU.is_equal))
            dve.tensor_tensor(hot, hot, over_e(valid), ALU.mult).then_inc(chosen, 1)
            dve.wait_ge(prefix_psum, 1)
            flat = "p e k -> p (e k)"
            glink(dve.tensor_copy(work_a.rearrange(flat), bank_pt[1][:, 0:KE]))
            glink(dve.tensor_tensor_scan(work_b.rearrange(flat), carry[:, :, :].rearrange(flat), work_a.rearrange(flat),
                                         0.0, ALU.mult, ALU.add))
            dve.tensor_tensor(work_a, work_b, work_a, ALU.subtract)
            glink(dve.tensor_copy(counts_i[:, :], work_b[:, :, 2 * B - 1]))
            glink(dve.tensor_scalar(counts_i[:, :], counts_i[:, :], 127.0, None, ALU.add))
            glink(dve.tensor_scalar(counts_i[:, :], counts_i[:, :], 7, None, ALU.arith_shift_right))
            glink(dve.tensor_copy(tiles_f[:, :], counts_i[:, :]))
            glink(dve.tensor_tensor_scan(ends[:, :], ones[:, 0:EXPERTS], tiles_f[:, :], 0.0, ALU.mult, ALU.add))
            glink(dve.tensor_tensor(base[:, :], ends[:, :], tiles_f[:, :], ALU.subtract))
            xe = [128, XT, EXPERTS]
            glink(dve.tensor_tensor(ended[:, :, :], iota_t[:, :].unsqueeze(2).to_broadcast(xe),
                                    ends[:, :].unsqueeze(1).to_broadcast(xe), ALU.is_ge))
            glink(dve.tensor_reduce(owner[:, :], ended[:, :, :], AX.X, ALU.add))
            dve.tensor_scalar(owner_i[:, :], owner[:, :], float(EXPERTS - 1), None, ALU.min)
            glink(dve.tensor_scalar(base[:, :], base[:, :], 128.0, None, ALU.mult))
            glink(dve.tensor_tensor(work_b.rearrange(flat), work_a.rearrange(flat), bank_pt[0][:, 0:KE], ALU.add))
            glink(dve.tensor_tensor(work_b, work_b, over_k(base), ALU.add))
            glink(dve.tensor_tensor(work_b, work_b, hot, ALU.mult))
            glink(dve.tensor_reduce(slot_f[:, :], work_b.rearrange(by_token), AX.X, ALU.add))
            dve.tensor_copy(slot_i[:, :], slot_f[:, :]).then_inc(slots_ready, 1)

            def expert_of(tile):
                return dve.value_load(owner_i[0:1, bass.ds(tile, 1)], min_val=0, max_val=EXPERTS - 1)

            def fetch(dst, w, e):
                dve.tensor_copy(dst[0], w[0][:, bass.ds(e * D, D)])
                return dve.tensor_copy(dst[1], w[1][:, bass.ds(e * D, D)])

            def expert_step(i, par):
                two = par % 2
                if real(i + 1, XT):
                    first = expert_of(i + 1)
                if real(i - 2, XT):
                    second = expert_of(i - 2)
                    dve.wait_ge(ehT_psum, i - 1)
                    dve.tensor_copy(ehT[two][0][:, :], bank_pt[two][:, 0:128])
                elif real(i, XT):
                    need(dve, eh_psum, i)
                if real(i + 1, XT):
                    fetch(tile_w[0][1 - two], ew1, first).then_inc(w1_fetched, 1)
                if real(i - 2, XT):
                    dve.tensor_copy(ehT[two][1][0:DB, :], bank_pt[two][0:DB, 128:256])
                    fetch(tile_w[1][two], ew2, second).then_inc(ehT_ready, 1)

            dve.wait_ge(e_loaded, 16 * 9)
            fetch(tile_w[0][0], ew1, expert_of(0)).then_inc(w1_fetched, 1)
            staged(dve, expert_step, (1, 4), XT, 4)
            for b in range(B):
                dve.wait_ge(back[b % 4], 32 * (b // 4 + 1))
                for t, rows in TILES:
                    r = resid[0:rows, b + 1, t, :]
                    ins = dve.tensor_tensor(r, r, xn4[0:rows, 2 * b + t, :], ALU.add)
                ins.then_inc(summed, 1)

        @block.tensor
        def _(pe):
            pe.wait_ge(scores_ready, 1)
            pe.wait_ge(consts, 1)
            pe.transpose(bank_out[0:2 * B, 0:128], tok_score[:, :], ident[:, :]).then_inc(scoresT_psum, 1)
            pe.sem_inc(picked, 2)
            with pe.Fori(0, B // 2) as i:
                for par in range(2):
                    b = 2 * i + par
                    pe.wait_ge(onehot_ready, b + 1)
                    pe.wait_ge(resid_ready, b + 1)
                    for t, rows in TILES:
                        for h in range(2):
                            ins = pe.matmul(bank_k[par][0:rows, t * D:(t + 1) * D],
                                            onehot[:, par, h, t * TA:t * TA + rows],
                                            x_all[:, bass.ds(2 * b + h, 1), :].rearrange("p o d -> p (o d)"),
                                            start=(h == 0), stop=(h == 1))
                    ins.then_inc(picked, 1)

            pe.wait_ge(w0_loaded, 16 * 18)
            pe.wait_ge(ws_ready, 2)
            pe.sem_inc(scored, 2)
            pe.sem_inc(turned, 1)

            def turn_tokens(bank, src):
                for r, (lo, hi) in enumerate(((0, DA), (DA, D))):
                    for t, rows in TILES:
                        ins = pe.transpose(bank[0:hi - lo, r * KEEP + t * TA:r * KEEP + t * TA + rows],
                                           src[0:rows, t, lo:hi], ident[0:rows, 0:rows])
                return ins

            def product(out, lhs, rhs):
                pe.matmul(out, lhs[0], rhs[0], start=True, stop=False)
                return pe.matmul(out, lhs[1], rhs[1], start=False, stop=True)

            def pre_turn(c):
                pe.wait_ge(normed_ready, c + 1)
                if not isinstance(c, int):
                    pe.wait_ge(v_ready, c)
                turn_tokens(bank_pre, normed).then_inc(xT_psum, 1)

            def pre_q_mm(c, par):
                pe.wait_ge(xT_ready, c + 1)
                x = (xT[0][:, :], xT[1][:, :])
                for h in range(2):
                    ins = product(bank_pre[:, h * KEEP:(h + 1) * KEEP], [w[:, 128 * h:128 * h + 128] for w in wq0], x)
                ins.then_inc(q_psum, 1)

            def pre_k_mm(c, par):
                x = (xT[0][:, :], xT[1][:, :])
                for h in range(2):
                    ins = product(bank_k[par][:, h * KEEP:(h + 1) * KEEP], [w[:, 128 * h:128 * h + 128] for w in wk0], x)
                ins.then_inc(k_psum, 1)

            def pre_v_mm(c):
                pe.wait_ge(q_ready, c + 1)
                for t, rows in TILES:
                    ins = product(bank_pre[0:rows, t * D:(t + 1) * D],
                                  [x[:, t * TA:t * TA + rows] for x in xT], [w[:, :] for w in wv0])
                ins.then_inc(v_psum, 1)

            def score_group(b, par, g):
                n = b * GROUPS + g
                slot = (par * GROUPS + g) % 2
                pe.wait_ge(tanh_done, n + 1)
                tanhs = arg_slot(par * GROUPS + g)[0]
                pe.wait_ge(smax_done, n + 1)
                for j in range(4):
                    for quad in range(4):
                        u = 4 * quad + j
                        if u < units(g):
                            ins = pe.matmul(bank_s[slot][32 * quad:32 * quad + 32, 0:KEEP], ws_place[:, j, :],
                                            tanhs[:, u * KEEP:(u + 1) * KEEP],
                                            start=(j == 0), stop=(j == 3 or u + 1 >= units(g)))
                ins.then_inc(scored, 1)

            def turn_group(b, par, g):
                n = b * GROUPS + g
                pslot = (par * GROUPS + g - 3) % 2
                bb, gg = (b, g - 3) if g >= 3 else (b - 1, g - 3 + GROUPS)
                c, k = gg // CHUNK, gg % CHUNK
                pe.wait_ge(exp_done, n + 2)
                if k == 0:
                    pe.wait_ge(pt_ready, CHUNKS * bb + c + 2)
                pe.transpose(bank_pt[0][:, 128 * k:128 * k + 128], p_sb[pslot][:, 0:TA], ident[:, :])
                pe.transpose(bank_pt[1][0:TB, 128 * k:128 * k + 128], p_sb[pslot][:, TA:KEEP],
                             ident[:, :]).then_inc(turned, 1)

            def head_cols(h, t0, rows):
                first, step = (h, 8) if h < 8 else (8 * UA + h - 8, 4)
                return slice(first + step * t0, first + step * (t0 + rows - 1) + 1, step)

            def context(b, par, heads):
                for h in heads:
                    for t, rows in TILES:
                        o = bank_out[0:rows, t * HEADS * VC + h * VC:t * HEADS * VC + (h + 1) * VC]
                        for s, srows in TILES:
                            ins = pe.matmul(o, pt[1 - par][s][0:srows, head_cols(h, t * TA, rows)],
                                            v_sb[1 - par][0:srows, s, h, :], start=(s == 0), stop=(s == 1))
                return ins

            def lagging(b, par, g, last=False):
                if not last or g < 3:
                    turn_group(b, par, g)
                if g == 4:
                    pe.wait_ge(pt_ready, CHUNKS * b + 2)
                if 4 <= g < 10:
                    ins = context(b, par, (2 * g - 8, 2 * g - 7))
                if g == 9:
                    ins.then_inc(ctx_psum, 1)
                if g == 11:
                    pe.wait_ge(ctx_ready, b + 1)
                    turn_tokens(bank_out, ctx_sb).then_inc(ctxT_psum, 1)
                if g == 13:
                    pe.wait_ge(ctxT_ready, b + 1)
                    for t, rows in TILES:
                        ins = product(bank_out[0:rows, t * D:(t + 1) * D],
                                      [x[:, t * TA:t * TA + rows] for x in ctxT], [w[:, :] for w in wo0])
                    ins.then_inc(proj_psum, 1)
                if last:
                    return
                if g == 1:
                    pre_turn(b + 1)
                if g == 10:
                    pre_q_mm(b + 1, 1 - par)
                if g == 12:
                    pre_k_mm(b + 1, 1 - par)
                if g == 14:
                    pre_v_mm(b + 1)

            pre_turn(0)
            pre_q_mm(0, 0)
            pre_k_mm(0, 0)
            pre_v_mm(0)
            with pe.Fori(0, B // 2) as i:
                for par in range(2):
                    b = 2 * i + par
                    for g in range(GROUPS):
                        score_group(b, par, g)
                        lagging(b, par, g)
            for g in range(GROUPS):
                lagging(B, 0, g, last=True)

            def ffn_step(i, par):
                if real(i + 1):
                    pe.wait_ge(f_normed, i + 2)
                    if not isinstance(i, int) or i >= 0:
                        pe.wait_ge(f_xT_ready, i + 1)
                    turn_tokens(bank_pre, fnorm[1 - par]).then_inc(f_xT_psum, 1)
                if real(i):
                    pe.wait_ge(f_xT_ready, i + 1)
                    if not isinstance(i, int) or i >= 2:
                        pe.wait_ge(gelu_done, i - 1)
                    for c in range(HT):
                        o = ffn_banks[par][c // 2][:, c % 2 * KEEP:(c % 2 + 1) * KEEP]
                        ins = product(o, [w[:, c * 128:(c + 1) * 128] for w in w1q], [x[:, :] for x in fx[par]])
                        if c % 2:
                            ins.then_inc(h_psum, 1)
                if real(i - 1):
                    b = i - 1
                    pe.wait_ge(hq_ready, b + 1)
                    if not isinstance(b, int) or b >= 1:
                        pe.wait_ge(f_added, b)
                    for t, rows in TILES:
                        for c in range(HT):
                            ins = pe.matmul(bank_out[0:rows, t * D:(t + 1) * D],
                                            hq[1 - par][:, c * KEEP + t * TA:c * KEEP + t * TA + rows], w2q[:, c, :],
                                            start=(c == 0), stop=(c == HT - 1))
                    ins.then_inc(y_psum, 1)

            pe.wait_ge(wq_step, 9)
            ffn_step(-1, 1)
            staged(pe, ffn_step, (1, 1))

            def xq_turn(c, par):
                pe.wait_ge(xq_ready, c + 1)
                need(pe, qkv_out, 4 * c)
                b16 = bank_pre.bitcast(BF16)
                for r, (lo, hi) in enumerate(((0, DA), (DA, D))):
                    for t, rows in TILES:
                        ins = pe.transpose(b16[0:hi - lo, r * 256 + t * TA:r * 256 + t * TA + rows],
                                           xq[par][0:rows, t, lo:hi], ident16[0:rows, 0:rows])
                ins.then_inc(xqT_psum, 1)

            def split_product(pairs):
                out, terms = pairs
                for n, (lhs, rhs) in enumerate(terms):
                    ins = pe.matmul(out, lhs, rhs, start=(n == 0), stop=(n == len(terms) - 1))
                return ins

            def qkv_mm(c, par, fill):
                if fill == 0:
                    pe.wait_ge(xqT_ready, c + 1)
                else:
                    pe.wait_ge(qkv_out, 4 * c + fill)
                x = xqT[par]
                if fill < 3:
                    for col in range(2):
                        kind, r = ((0, col), (1, col), (col, 2))[fill]
                        ins = split_product((bank_pre[:, col * KEEP:(col + 1) * KEEP],
                                             [(w1parts[kind][m][h][:, 128 * r:128 * r + 128], x[h][:, :])
                                              for m in range(3) for h in range(2)]))
                else:
                    for t, rows in TILES:
                        ins = split_product((bank_pre[0:rows, t * D:(t + 1) * D],
                                             [(x[h][:, t * TA:t * TA + rows], w1parts[2][m][h][:, :])
                                              for m in range(3) for h in range(2)]))
                ins.then_inc(qkv_psum, 1)

            def context1(b, par, r, col):
                for s, srows in TILES:
                    for j in range(4):
                        h = 4 * r + j
                        ins = pe.matmul(bank_out[32 * j:32 * j + 32, col * KEEP:(col + 1) * KEEP],
                                        v1[par][0:srows, s, h, :], pt1[par][s][0:srows, h * KEEP:(h + 1) * KEEP],
                                        start=(s == 0), stop=(s == 1))
                return ins

            def context1_turn(b, lo, hi, k):
                pe.wait_ge(ctx1_out, 2 * b + k + 1)
                n = hi - lo
                for t, rows in TILES:
                    for r in range(lo, hi):
                        c = t * 128 * n + (r - lo) * 128
                        ins = pe.transpose(bank_out[0:rows, c:c + 128],
                                           ctx1[:, r * KEEP + t * TA:r * KEEP + t * TA + rows], ident[:, :])
                ins.then_inc(ctx1_tokens, 1)

            def attn1_step(b, par):
                for u in range(PAIRS):
                    n, slot = PAIRS * b + u, u % 2
                    if u == 2 and real(b - 5):
                        need(pe, pair_scaled, min(n - 1, PAIRS * B) if isinstance(n, int) else n - 1)
                        pe.wait_ge(gxT_ready, b - 4)
                        need(pe, gate_out, b - 5)
                        for t, rows in TILES:
                            ins = product(bank_k0[0:rows, 2 * KEEP + t * EXPERTS:2 * KEEP + (t + 1) * EXPERTS],
                                          [x[:, t * TA:t * TA + rows] for x in xT], [w[:, :] for w in wg])
                        ins.then_inc(gate_psum, 1)
                    if real(n, PAIRS * B):
                        if u == 0:
                            pe.wait_ge(qkv_out, 4 * b + 3)
                        need(pe, pair_scaled, n - 1)
                        for t in range(2):
                            for e in range(2):
                                r, j = (2 * u + e) // 4, (2 * u + e) % 4
                                ins = pe.matmul(pair_banks[slot][:, e, t, :],
                                                q1[par][32 * j:32 * j + 32, r, t * TA:(t + 1) * TA],
                                                k1[par][32 * j:32 * j + 32, r, :], start=True, stop=True)
                        ins.then_inc(pair_scored, 1)
                    m = n - 2
                    if real(m, PAIRS * B):
                        pe.wait_ge(pair_powered, m + 1)
                        need(pe, pair_pt, m)
                        p = p1[slot].rearrange("p (e t s) -> p e t s", e=2, t=2)
                        for e in range(2):
                            for s, srows in TILES:
                                for t, rows in TILES:
                                    c = e * KEEP + t * TA
                                    ins = pe.transpose(bank_pt[s][0:srows, c:c + rows],
                                                       p[0:rows, e, t, s * TA:s * TA + srows], ident[0:rows, 0:rows])
                        ins.then_inc(pair_turned, 1)
                    if real(b - 1):
                        if u == 0:
                            need(pe, added1, b - 1)
                            pe.wait_ge(pair_pt, PAIRS * (b - 1) + 4)
                            pe.wait_ge(qkv_out, 4 * b)
                            context1(b - 1, 1 - par, 0, 0)
                            context1(b - 1, 1 - par, 1, 1).then_inc(ctx1_psum, 1)
                        if u == 1:
                            context1_turn(b - 1, 0, 2, 0)
                        if u == 2:
                            pe.wait_ge(pair_pt, PAIRS * b)
                            pe.wait_ge(ctx1_ready, 2 * b - 1)
                            context1(b - 1, 1 - par, 2, 0).then_inc(ctx1_psum, 1)
                        if u == 3:
                            context1_turn(b - 1, 2, 3, 1)
                        if u == 4:
                            pe.wait_ge(ctx1_ready, 2 * b)
                            turn_tokens(bank_out, ctx_sb).then_inc(ctx1T_psum, 1)
                        if u == 5:
                            pe.wait_ge(ctx1T_ready, b)
                            for t, rows in TILES:
                                ins = product(bank_out[0:rows, t * D:(t + 1) * D],
                                              [x[:, t * TA:t * TA + rows] for x in ctxT], [w[:, :] for w in wo1])
                            ins.then_inc(proj1_psum, 1)
                    if u == 0 and real(b - 5):
                        pe.wait_ge(n4_ready, b - 4)
                        pe.wait_ge(qkv_out, 4 * b + 4 if not isinstance(b, int) else min(4 * b + 4, 4 * B))
                        turn_tokens(bank_pre, fnorm[1 - par]).then_inc(gxT_psum, 1)
                    if real(b + 1):
                        if u == 1:
                            if real(b - 5):
                                pe.wait_ge(gxT_ready, b - 4)
                            xq_turn(b + 1, 1 - par)
                        if u >= 2:
                            qkv_mm(b + 1, 1 - par, u - 2)

            pe.wait_ge(w1_ready, 1)
            pe.wait_ge(w1_loaded, 16 * 18)
            xq_turn(0, 0)
            for fill in range(4):
                qkv_mm(0, 0, fill)
            pe.wait_ge(e_loaded, 16 * 3)
            staged(pe, attn1_step, (1, 5))

            pe.wait_ge(chosen, 1)
            hot = gate[1].rearrange("p e k -> p (e k)")
            pe.matmul(bank_pt[0][:, 0:KE], lower[:, :], hot, start=True, stop=True)
            pe.matmul(bank_pt[1][:, 0:KE], ones[:, :], hot, start=True, stop=True).then_inc(prefix_psum, 1)

            def turn_tile(bank, src):
                pe.transpose(bank[:, 0:128], src[:, 0:DA], ident[:, :])
                return pe.transpose(bank[0:DB, 128:256], src[:, DA:D], ident[:, :])

            pe.wait_ge(slots_ready, 1)

            def expert_step(i, par):
                two = par % 2
                if real(i, XT):
                    pe.wait_ge(xs_loaded[par], 4 * (i - par) + 16)
                    need(pe, exT_ready, i - 1)
                    turn_tile(bank_k[two], xs[par]).then_inc(exT_psum, 1)
                if real(i - 1, XT):
                    pe.wait_ge(exT_ready, i)
                    pe.wait_ge(w1_fetched, i)
                    need(pe, eh_ready, i - 2)
                    product(bank_s[1 - two][:, 0:D], [x[:, :] for x in exT[1 - two]], tile_w[0][1 - two]).then_inc(eh_psum, 1)
                if real(i - 2, XT):
                    pe.wait_ge(eh_ready, i - 1)
                    need(pe, ehT_ready, i - 3)
                    turn_tile(bank_pt[two], eh[two]).then_inc(ehT_psum, 1)
                if real(i - 3, XT):
                    pe.wait_ge(ehT_ready, i - 2)
                    need(pe, ey_ready, i - 4)
                    product(out_banks[1 - two][:, 0:D], [x[:, :] for x in ehT[1 - two]], tile_w[1][1 - two]).then_inc(ey_psum, 1)

            staged(pe, expert_step, (0, 8), XT, 4)


_TURNED = ["L0_attn_Wq", "L0_attn_Wk", "L0_attn_Wv", "L0_attn_Wo", "L0_ffn_W1", "L0_ffn_W2",
           "L1_ffn_W1", "L1_ffn_W2", "L1_ffn_Wg"]
_COLS = {"L0_ffn_b1": 128, "L1_attn_bq": 4 * HD, "L1_attn_bk": 4 * HD}
_INS = ["x", "L0_tok_w", "L0_tok_b", "L0_attn_bq", "L0_attn_bk", "L0_attn_bv", "L0_attn_bo", "L0_attn_ws", "L0_attn_bs",
        "L0_ffn_b2", "L0_ffn_s_gelu", "L0_ffn_s_out",
        "L1_attn_Wq", "L1_attn_Wk", "L1_attn_Wv", "L1_attn_Wo", "L1_attn_bv", "L1_attn_bo",
        "L1_ffn_b1", "L1_ffn_b2", "L1_ffn_bg"]


def kernel(**inputs):
    import numpy as _np
    import concourse.bacc as _bacc
    from concourse import mybir as _mybir
    from concourse.bass_utils import run_bass_kernel_spmd as _run

    nc = _bacc.Bacc("TRN2", target_bir_lowering=False, num_devices=1)
    arrays, aps = {}, {}
    for name in _INS + _TURNED + list(_COLS):
        a = _np.asarray(inputs[name])
        if name in _COLS:
            a = a.reshape(-1, _COLS[name]).T
            name += "_cols"
        if name in _TURNED:
            a = _np.swapaxes(a, -1, -2)
            name += "T"
        a = _np.ascontiguousarray(a)
        arrays[f"in_{name}"] = a
        aps[name] = nc.dram_tensor(f"in_{name}", a.shape, _mybir.dt.from_np(a.dtype), kind="ExternalInput").ap()
    out = nc.dram_tensor("out", (B, KEEP, D), F32, kind="ExternalOutput").ap()
    build(nc, aps, out)
    r = _run(nc, [arrays], core_ids=[0])
    return r.results[0]["out"]
```
